# Optimizing a Trainium2 kernel written in Bass

```python
import numpy as np
import jax
import jax.numpy as jnp

def _softmax(x, axis=-1):
    return jax.nn.softmax(x, axis=axis)

def _gelu(x):
    return jax.nn.gelu(x, approximate=True)

def _silu(x):
    return jax.nn.silu(x)

def _sigmoid(x):
    return jax.nn.sigmoid(x)

def _layernorm(x, axis=-1, eps=1e-05):
    m = jnp.mean(x, axis=axis, keepdims=True)
    v = jnp.var(x, axis=axis, keepdims=True)
    return (x - m) / jnp.sqrt(v + eps)

def _scatter_add(tgt, idx, src, axis=0):
    return tgt.at[idx].add(src)

def _segment_sum(src, seg, n):
    return jax.ops.segment_sum(src, seg, n)
kernel_name = 'mk_adj_preln_d2_adj_r2_31dd20'

def setup_inputs(seed: int=0):
    np.random.seed(seed)
    _w = jnp.asarray

    def _rec_inputs():
        import jax
        import jax.numpy as jnp
        _gk = jax.random.key(seed)
        x = 0.0001732 + 1 * jax.random.normal(jax.random.fold_in(_gk, 1), (5120, 64), jnp.float32)
        _a = jax.random.bernoulli(jax.random.fold_in(_gk, 2), 0.003125, (5120, 5120))
        _af = _a.astype(jnp.float32)
        _af = _af * jax.random.uniform(jax.random.fold_in(_gk, 3), (5120, 5120), jnp.float32, 0.05, 0.02)
        adj = _af
        return (x, adj)
    x, adj = _rec_inputs()

    def _L0_gnn_setup():
        import jax, jax.numpy as jnp
        import numpy as np
        N_USERS = 2048
        N_ITEMS = 3072
        EMB = 64
        LN_EPS = 1e-05
        key = jax.random.key(seed)
        ks = jax.random.split(key, 10)
        N = N_USERS + N_ITEMS
        ego = jax.random.normal(ks[0], (N, EMB), jnp.float32)
        adj = (jax.random.uniform(ks[1], (N, N), jnp.float32) < 0.01).astype(jnp.float32) * 0.02
        xav = float(np.sqrt(6.0 / (EMB + EMB)))
        W_u = jax.random.uniform(ks[2], (EMB, EMB), jnp.float32, -xav, xav)
        W_i = jax.random.uniform(ks[3], (EMB, EMB), jnp.float32, -xav, xav)
        diag_u = jax.random.uniform(ks[4], (N_USERS,), jnp.float32, 0.99, 1.01)
        diag_i = jax.random.uniform(ks[5], (N_ITEMS,), jnp.float32, 0.99, 1.01)
        par_u = jax.random.uniform(ks[6], (2,), jnp.float32, 0.0, 0.99)
        par_i = jax.random.uniform(ks[7], (2,), jnp.float32, 0.0, 0.99)
        ln_gamma = jnp.ones((EMB,), jnp.float32)
        ln_beta = jnp.zeros((EMB,), jnp.float32)
        return {'ego_embeddings': ego, 'adj': adj, 'W_u': W_u, 'diag_u': diag_u, 'par_u': par_u, 'W_i': W_i, 'diag_i': diag_i, 'par_i': par_i, 'ln_gamma': ln_gamma, 'ln_beta': ln_beta}
    _L0_gnn_all = _L0_gnn_setup()
    _L0_gnn_in = {k: v for k, v in _L0_gnn_all.items() if k in ('W_u', 'diag_u', 'par_u', 'W_i', 'diag_i', 'par_i', 'ln_gamma', 'ln_beta')}
    del _L0_gnn_all

    def _L1_gnn_setup():
        import jax, jax.numpy as jnp
        import numpy as np
        N, IN_F, OUT_F, K = (8192, 64, 64, 4)
        key = jax.random.key(seed)
        k1, k2, k3 = jax.random.split(key, 3)
        x = jax.random.normal(k1, (N, IN_F), dtype=jnp.float32)
        L_scaled = jax.random.normal(k2, (N, N), dtype=jnp.float32) / np.sqrt(N)
        fan_in, fan_out = (K * IN_F, OUT_F)
        bound = np.sqrt(6.0 / (fan_in + fan_out))
        weight = jax.random.uniform(k3, (K, IN_F, OUT_F), dtype=jnp.float32, minval=-bound, maxval=bound)
        bias = jnp.zeros((OUT_F,), dtype=jnp.float32)
        return {'x': x, 'L_scaled': L_scaled, 'weight': weight, 'bias': bias}
    _L1_gnn_all = _L1_gnn_setup()
    _L1_gnn_in = {k: v for k, v in _L1_gnn_all.items() if k in ('weight', 'bias')}
    del _L1_gnn_all
    return {'x': x, 'adj': adj, 'L0_gnn_W_u': _L0_gnn_in['W_u'], 'L0_gnn_diag_u': _L0_gnn_in['diag_u'], 'L0_gnn_par_u': _L0_gnn_in['par_u'], 'L0_gnn_W_i': _L0_gnn_in['W_i'], 'L0_gnn_diag_i': _L0_gnn_in['diag_i'], 'L0_gnn_par_i': _L0_gnn_in['par_i'], 'L0_gnn_ln_gamma': _L0_gnn_in['ln_gamma'], 'L0_gnn_ln_beta': _L0_gnn_in['ln_beta'], 'L1_gnn_weight': _L1_gnn_in['weight'], 'L1_gnn_bias': _L1_gnn_in['bias']}

def reference(x, adj, L0_gnn_W_u, L0_gnn_diag_u, L0_gnn_par_u, L0_gnn_W_i, L0_gnn_diag_i, L0_gnn_par_i, L0_gnn_ln_gamma, L0_gnn_ln_beta, L1_gnn_weight, L1_gnn_bias):
    import jax
    import jax.numpy as jnp

    def _L0_gnn_ref(ego_embeddings, adj, W_u, diag_u, par_u, W_i, diag_i, par_i, ln_gamma, ln_beta):
        import jax, jax.numpy as jnp
        import numpy as np
        N_USERS = 2048
        N_ITEMS = 3072
        EMB = 64
        LN_EPS = 1e-05
        nu = diag_u.shape[0]
        res = ego_embeddings
        ego_u = ego_embeddings[:nu]
        ego_i = ego_embeddings[nu:]
        u = par_u[0] * par_u[1] * (diag_u[:, None] * ego_u @ W_u) + ego_u
        i = par_i[0] * par_i[1] * (diag_i[:, None] * ego_i @ W_i) + ego_i
        e = jnp.concatenate([u, i], axis=0)
        h = adj @ (adj.T @ e)
        mu = jnp.mean(h, axis=-1, keepdims=True)
        var = jnp.var(h, axis=-1, keepdims=True)
        out = (h - mu) * jax.lax.rsqrt(var + LN_EPS) * ln_gamma + ln_beta + res
        return out

    def _L1_gnn_ref(x, L_scaled, weight, bias):
        import jax, jax.numpy as jnp
        import numpy as np
        N, IN_F, OUT_F, K = (8192, 64, 64, 4)
        Tx_prev2 = x
        Tx_prev1 = L_scaled @ x
        out = Tx_prev2 @ weight[0]
        if K > 1:
            out = out + Tx_prev1 @ weight[1]
        for k in range(2, K):
            Tx_curr = 2.0 * (L_scaled @ Tx_prev1) - Tx_prev2
            out = out + Tx_curr @ weight[k]
            Tx_prev2, Tx_prev1 = (Tx_prev1, Tx_curr)
        return out + bias
    h = jnp.maximum(_layernorm(x, axis=-1), 0.0)
    x = x + _L0_gnn_ref(h, adj, L0_gnn_W_u, L0_gnn_diag_u, L0_gnn_par_u, L0_gnn_W_i, L0_gnn_diag_i, L0_gnn_par_i, L0_gnn_ln_gamma, L0_gnn_ln_beta)
    h = jnp.maximum(_layernorm(x, axis=-1), 0.0)
    x = x + _L1_gnn_ref(h, adj, L1_gnn_weight, L1_gnn_bias)
    return x

_drawn_inputs = setup_inputs


def setup_inputs(seed=0):
    import zlib

    import numpy as np

    out = dict(_drawn_inputs(seed))
    spreads = {'L0_gnn_ln_gamma': (1.0, 0.2), 'L0_gnn_ln_beta': (0.0, 0.1), 'L1_gnn_bias': (0.0, 0.1)}
    factors = {}
    for name, (base, spread) in spreads.items():
        noise = np.random.default_rng([zlib.crc32(name.encode()), seed]).standard_normal(out[name].shape)
        drawn = base * np.exp(spread * noise) if base else spread * noise
        out[name] = jnp.asarray(drawn.astype(out[name].dtype))
    for name, factor in factors.items():
        out[name] = (out[name] * factor).astype(out[name].dtype)
    return out
```

```python
import concourse.bass as bass
from concourse import mybir
from contextlib import ExitStack

F32 = mybir.dt.float32
F32R = mybir.dt.float32r
ALU = mybir.AluOpType
ACT = mybir.ActivationFunctionType

P = 128
N = 5120
D = 64
NT = N // P
NU = 2048
RB = 512
NB = N // RB
TB = RB // P
CW = 256
CR = 1024
CA = N // CR
NJ = N // CW
SA = CA * 4
OCT = 8
NO = NT // OCT
EPS = 1e-5
ACC = RB // P * CW

S_B = NJ * SA
S_C = S_B + NB * NB * 4
S_D = S_C + NB * (NB + 1) // 2 * 4
S_END = S_D + NB * (NB + 1) // 2 * 4


def build(nc, x, adj, W_u, diag_u, par_u, W_i, diag_i, par_i, gamma, beta, weight, bias, out):
    ctx = ExitStack()
    with ctx:
        def sb(name, shape, dt=F32):
            return ctx.enter_context(nc.sbuf_tensor(name, shape, dt))

        def pb(name, shape):
            return ctx.enter_context(nc.psum_tensor(name, shape, F32))

        def sem(name):
            return ctx.enter_context(nc.semaphore(name))

        nat = sb("nat", [P, NB, 2048])
        rowwise = ExitStack()
        hT = rowwise.enter_context(nc.sbuf_tensor("hT", [D, OCT * P], F32))
        tmp = rowwise.enter_context(nc.sbuf_tensor("tmp", [P, OCT, D], F32))
        T0 = rowwise.enter_context(nc.sbuf_tensor("T0", [P, 2, OCT, D], F32))
        stats = rowwise.enter_context(nc.sbuf_tensor("stats", [P, 2, 2, OCT, 6], F32))
        w_ui = rowwise.enter_context(nc.sbuf_tensor("w_ui", [D, 2, D], F32))
        dg_row = rowwise.enter_context(nc.sbuf_tensor("dg_row", [NT, P], F32))
        rowwise.close()
        hi = sb("hi", [P, 4, RB], F32R)
        lo = sb("lo", [P, 4, RB], F32R)
        vw_hi = sb("vw_hi", [P, NT, P], F32R)
        vw_lo = sb("vw_lo", [P, NT, P], F32R)
        outacc = sb("outacc", [P, NT, D])
        part = sb("part", [P, NT, D])
        ident = sb("ident", [P, P])
        r_sum = sb("r_sum", [P, D])
        r_B = sb("r_B", [P, 3 * D])
        r_C = sb("r_C", [P, 2 * D])
        r_D = sb("r_D", [P, D])
        w_0 = sb("w_0", [D, D])
        wk = sb("wk", [P, 4, D])
        vecs = sb("vecs", [P, 3, D])
        par = sb("par", [P, 2, 2])
        pd = sb("pd", [P, NT])
        par_p = sb("par_p", [P, 2])
        eps = sb("eps", [P, 1])
        tT = sb("tT", [P, 2, 2, P], F32R)
        accS = sb("accS", [P, RB])
        mv = sb("mv", [P, 2, 2, OCT, 2])
        rs = sb("rs", [P, 2, 2, OCT])
        nmr = sb("nmr", [P, 2, 2, OCT])
        std = sb("std", [P, 2, 2, OCT])
        t2 = sb("t2", [P, TB, D])
        early = ExitStack()

        hacc = early.enter_context(nc.sbuf_tensor("hacc", [P, N], F32))
        evec = early.enter_context(nc.sbuf_tensor("evec", [P, NT, D], F32))
        h0 = early.enter_context(nc.sbuf_tensor("h0", [P, NT, D], F32))
        early.close()
        uw_hi = sb("uw_hi", [P, NT, P], F32R)
        uw_lo = sb("uw_lo", [P, NT, P], F32R)
        xin = outacc

        psT = pb("psT", [P, 4, RB])
        acc = pb("acc", [P, 2, RB])
        fin = pb("fin", [P, 2 * RB])

        loaded = [sem(f"loaded{s}") for s in range(NB)]
        slot_used = [sem(f"slot_used{s}") for s in range(NB)]
        x_in, par_in, w_in = sem("x_in"), sem("par_in"), sem("w_in")
        const_ready, consts = sem("const_ready"), sem("consts")
        pd_t, pd_ready = sem("pd_t"), sem("pd_ready")
        dchain, pchain = sem("dchain"), sem("pchain")
        transposed, hi_ready, lo_ready, strip_used = (
            sem("transposed"), sem("hi_ready"), sem("lo_ready"), sem("strip_used"))
        t_ready, t_hi, t_split = sem("t_ready"), sem("t_hi"), sem("t_split")
        acc_free = sem("acc_free")
        mean1, std1, rs1, h0_ready, h0_t, h0_tc, h0_w, e_ready = (sem(n) for n in (
            "mean1", "std1", "rs1", "h0_ready", "h0_t", "h0_tc", "h0_w", "e_ready"))
        xr_ready = sem("xr_ready")
        h_row, mean2, std2, rs2, hn_ready, x1_ready, std3, rs3, T0_ready, T0_hi, T0_t, T0_tc, T0_w, T0_lo, T0_out = (
            sem(n) for n in ("h_row", "mean2", "std2", "rs2", "hn_ready", "x1_ready", "std3", "rs3", "T0_ready",
                             "T0_hi", "T0_t", "T0_tc", "T0_w", "T0_lo", "T0_out"))
        uw_zeroed = sem("uw_zeroed")
        acc_copied, fin_ready, fin_a, fin_v, rows_hi, rows_ready, uw_ready, t2_ready, t2_copied = (sem(n) for n in (
            "acc_copied", "fin_ready", "fin_a", "fin_v", "rows_hi", "rows_ready", "uw_ready", "t2_ready",
            "t2_copied"))
        out_ready, out_sent = sem("out_ready"), sem("out_sent")

        def f32(ap):
            return ap.bitcast(F32)

        fin4 = fin[:, :].rearrange("p (m c) -> p m c", m=TB)
        out_v = out.rearrange("(t p) d -> p t d", p=P)
        x_v = x.rearrange("(t p) d -> p t d", p=P)

        block = ctx.enter_context(nc.Block())

        @block.sync
        def _(sp):
            sp.dma_start(xin[:, :, :], x_v).then_inc(x_in, 16)
            sp.dma_start(w_ui[:, 0, :], W_u).then_inc(w_in, 16)
            sp.dma_start(w_ui[:, 1, :], W_i).then_inc(w_in, 16)
            sp.dma_start(wk[0:D, :, :], weight.rearrange("k i o -> i k o")).then_inc(w_in, 16)
            sp.dma_start(wk[D:P, :, :], weight.rearrange("k i o -> i k o")).then_inc(w_in, 16)
            adj_a = adj.rearrange("(c m p) n -> c p m n", p=P, m=CR // P)
            adj_b = adj.rearrange("(i m p) n -> i p m n", p=P, m=TB)

            def slot_left(slot, uses):
                sp.lower_val(uses)
                sp.wait_ge(w_in, 64)
                sp.wait_ge(slot_used[slot], uses)

            def load_a(slot, c, col, uses=None):
                dst = nat[:, slot, :].rearrange("p (m n) -> p m n", n=CW)
                src = adj_a[c, :, :, bass.ds(col, CW)]
                if uses is not None:
                    slot_left(slot, uses)
                sp.dma_start(dst, src).then_inc(loaded[slot], 16)

            def load_b(j, row, uses):
                dst = nat[:, j, :].rearrange("p (m n) -> p m n", n=RB)
                src = adj[bass.ds(row, RB), j * RB:(j + 1) * RB].rearrange("(m p) n -> p m n", p=P)
                slot_left(j, uses)
                sp.dma_start(dst, src).then_inc(loaded[j], 16)

            for slot in range(NB):
                load_a(slot, slot % CA, slot // CA * CW)
            with sp.Fori(1, NJ // 2) as it:
                for slot in range(NB):
                    load_a(slot, slot % CA, it * (2 * CW) + slot // CA * CW, it)
            with sp.Fori(0, NB) as r:
                for j in reversed(range(NB)):
                    load_b(j, r * RB, r + NB)
            with sp.Fori(0, NB) as r:
                row = (NB - 1) * RB - r * RB
                load_b(NB - 1, row, r + 2 * NB)
                for j in reversed(range(NB - 1)):
                    with sp.If(r > NB - 2 - j):
                        load_b(j, row, r + (NB + 1 + j))
                    sp.end_ifs()
            with sp.Fori(0, NB) as r:
                row, uses = sp.snap(r * RB), sp.snap(r + 2 * NB + 1)
                load_b(0, row, uses)
                for j in range(1, NB):
                    with sp.If(r > j - 1):
                        load_b(j, row, uses)
                    sp.end_ifs()

        @block.gpsimd
        def _(pool):
            nc.gpsimd.memset(ident[:, :], 0.0).then_inc(pchain, 1)
            nc.gpsimd.memset(eps[:, :], EPS).then_inc(const_ready, 1)
            pool.wait_ge(pchain, 1)
            nc.gpsimd.affine_select(out=ident[:, :], in_=ident[:, :], compare_op=ALU.not_equal, fill=1.0, base=0,
                                    pattern=[[-1, P]], channel_multiplier=1).then_inc(const_ready, 1)
            nc.gpsimd.memset(hacc[:, 0:N // 2], 0.0).then_inc(acc_free, 1)
            nc.gpsimd.memset(hacc[:, N // 2:N], 0.0).then_inc(acc_free, 1)
            nc.gpsimd.memset(r_B[:, :], 0.0).then_inc(pchain, 1)
            nc.gpsimd.memset(r_C[:, :], 0.0).then_inc(pchain, 1)
            nc.gpsimd.memset(f32(vw_hi[:, :, D:P]), 0.0).then_inc(pchain, 1)
            nc.gpsimd.memset(f32(vw_lo[:, :, D:P]), 0.0).then_inc(pchain, 1)
            pool.wait_ge(const_ready, 2)
            pool.wait_ge(pchain, 5)
            pool.wait_ge(w_in, 64)
            for h in (slice(0, D), slice(D, P)):
                nc.gpsimd.tensor_copy(r_sum[h, :], ident[h, h]).then_inc(consts, 1)
            nc.gpsimd.tensor_copy(r_B[0:D, 0:D], ident[0:D, 0:D]).then_inc(consts, 1)
            nc.gpsimd.tensor_copy(r_B[D:P, 2 * D:3 * D], ident[D:P, D:P]).then_inc(consts, 1)
            nc.gpsimd.tensor_copy(r_C[D:P, 0:D], ident[D:P, D:P]).then_inc(consts, 1)
            nc.gpsimd.tensor_tensor(r_B[0:D, D:2 * D], wk[0:D, 1, :], wk[0:D, 3, :], ALU.subtract).then_inc(consts, 1)
            nc.gpsimd.tensor_tensor(w_0[:, :], wk[0:D, 0, :], wk[0:D, 2, :], ALU.subtract).then_inc(consts, 1)
            nc.gpsimd.tensor_tensor(r_B[D:P, D:2 * D], wk[D:P, 2, :], wk[D:P, 2, :], ALU.add).then_inc(consts, 1)
            nc.gpsimd.tensor_tensor(r_C[D:P, D:2 * D], wk[D:P, 2, :], wk[D:P, 2, :], ALU.add).then_inc(consts, 1)
            nc.gpsimd.tensor_tensor(r_C[0:D, D:2 * D], wk[0:D, 3, :], wk[0:D, 3, :], ALU.add).then_inc(consts, 1)
            pool.wait_ge(consts, 10)
            nc.gpsimd.tensor_tensor(r_D[:, :], wk[:, 3, :], wk[:, 3, :], ALU.add).then_inc(consts, 1)
            pool.wait_ge(x_in, 16)
            pool.wait_ge(par_in, 16 * 7)
            pool.wait_ge(h0_ready, NO)
            nc.gpsimd.tensor_tensor(part[:, :, :], xin[:, :, :], h0[:, :, :], ALU.add).then_inc(pchain, 1)
            pool.wait_ge(pchain, 6)
            nc.gpsimd.tensor_tensor(part[:, :, :], part[:, :, :],
                                    vecs[:, 1:2, :].to_broadcast([P, NT, D]), ALU.add).then_inc(xr_ready, 1)
            pool.wait_ge(h_row, NO)
            nc.gpsimd.memset(f32(uw_hi[:, :, 0:D]), 0.0).then_inc(uw_zeroed, 1)
            nc.gpsimd.memset(f32(uw_lo[:, :, 0:D]), 0.0).then_inc(uw_zeroed, 1)
            with pool.Fori(0, NB) as r:
                pool.wait_ge(rows_ready, r + 1)
                rows = bass.ds(r * TB, TB)
                nc.gpsimd.tensor_copy(uw_hi[:, rows, D:P], f32(vw_hi[:, rows, D:P])).then_inc(uw_ready, 1)
                nc.gpsimd.tensor_copy(uw_lo[:, rows, D:P], f32(vw_lo[:, rows, D:P])).then_inc(uw_ready, 1)
            with pool.Fori(0, NB) as r:
                pool.wait_ge(rows_ready, r + NB + 1)
                rows = bass.ds((NB - 1) * TB - r * TB, TB)
                nc.gpsimd.tensor_copy(vw_hi[:, rows, 0:D], f32(uw_hi[:, rows, 0:D])).then_inc(t2_copied, 1)
                nc.gpsimd.tensor_copy(vw_hi[:, rows, D:P], f32(uw_lo[:, rows, 0:D])).then_inc(t2_copied, 1)
            with pool.Fori(0, NB) as r:
                pool.wait_ge(out_ready, r + 1)
                rows = bass.ds(r * TB, TB)
                pool.dma_start(out[bass.ds(r * RB, RB), :].rearrange("(m p) d -> p m d", p=P),
                               outacc[:, rows, :]).then_inc(out_sent, 16)
            pool.wait_ge(out_sent, 16 * NB)

        @block.scalar
        def _(act):
            act.dma_start(dg_row[0:NU // P, :], diag_u.rearrange("(t p) -> t p", p=P)).then_inc(par_in, 16)
            act.dma_start(dg_row[NU // P:NT, :], diag_i.rearrange("(t p) -> t p", p=P)).then_inc(par_in, 16)
            for n, v in enumerate((par_u, par_i)):
                act.dma_start(par[:, n, :], v.rearrange("(a n) -> a n", a=1).to_broadcast([P, 2])).then_inc(par_in, 16)
            for n, v in enumerate((gamma, beta, bias)):
                act.dma_start(vecs[:, n, :], v.rearrange("(a n) -> a n", a=1).to_broadcast([P, D])).then_inc(par_in, 16)

            act.wait_ge(const_ready, 2)
            for step in range(NO + 4):
                if step < NO:
                    o, b = step, step % 2
                    act.wait_ge(mean1, o + 1)
                    nc.scalar.activation(std[:, 0, b, :], mv[:, 0, b, :, 1], ACT.Sqrt, bias=eps[:, :]).then_inc(std1, 1)
                o = step - 1
                if 0 <= o < NO:
                    act.wait_ge(rs1, o + 1)
                    for m in range(OCT):
                        last = nc.scalar.activation(h0[:, o * OCT + m, :], xin[:, o * OCT + m, :], ACT.Relu,
                                                    bias=nmr[:, 0, o % 2, m:m + 1], scale=rs[:, 0, o % 2, m:m + 1])
                    last.then_inc(h0_ready, 1)
                o = step - 2
                if 0 <= o < NO:
                    act.wait_ge(h0_t, o + 1)
                    if o:
                        act.wait_ge(h0_w, o)
                    nc.scalar.activation(hT[:, :], acc[0:D, :, :].rearrange("p a b -> p (a b)"),
                                         ACT.Copy).then_inc(h0_tc, 1)

            def hi_strip(s, k):
                act.wait_ge(transposed, s + 1)
                act.wait_ge(strip_used, s - 3)
                nc.scalar.activation(hi[:, k, :], psT[:, k, :], ACT.Copy).then_inc(hi_ready, 1)

            tp = fin[:, :].rearrange("p (j c) -> p j c", j=2)

            def t_high(j, b):
                act.wait_ge(t_ready, j)
                nc.scalar.activation(tT[:, b, :, 0:D], tp[:, :, 0:D], ACT.Copy).then_inc(t_hi, 1)

            t_high(1, 0)
            for k in range(4):
                act.wait_ge(transposed, k + 1)
                nc.scalar.activation(hi[:, k, :], psT[:, k, :], ACT.Copy).then_inc(hi_ready, 1)

            def block_a(j, b, final=False):
                with act.Fori(0, CA - 1) as c:
                    for k in range(4):
                        hi_strip(j * SA + c * 4 + 4 + k, k)
                if not final:
                    t_high(j + 2, 1 - b)
                    for k in range(4):
                        hi_strip(j * SA + SA + k, k)

            with act.Fori(0, NJ // 2 - 1) as it:
                block_a(it * 2, 0)
                block_a(it * 2 + 1, 1)
            block_a(NJ - 2, 0)
            block_a(NJ - 1, 1, final=True)

            for step in range(NO + 5):
                o, b = step, step % 2
                if o < NO:
                    act.wait_ge(mean2, o + 1)
                    nc.scalar.activation(std[:, 0, b, :], mv[:, 0, b, :, 1], ACT.Sqrt, bias=eps[:, :]).then_inc(std2, 1)
                o = step - 1
                if 0 <= o < NO:
                    act.wait_ge(rs2, o + 1)
                    if o:
                        act.wait_ge(x1_ready, o)
                    for m in range(OCT):
                        last = nc.scalar.activation(tmp[:, m, :], psT[:, o % 4, m * D:(m + 1) * D], ACT.Identity,
                                                    bias=nmr[:, 0, o % 2, m:m + 1], scale=rs[:, 0, o % 2, m:m + 1])
                    last.then_inc(hn_ready, 1)
                o = step - 2
                if 0 <= o < NO:
                    act.wait_ge(x1_ready, o + 1)
                    nc.scalar.activation(std[:, 1, o % 2, :], mv[:, 1, o % 2, :, 1], ACT.Sqrt,
                                         bias=eps[:, :]).then_inc(std3, 1)
                o = step - 3
                if 0 <= o < NO:
                    act.wait_ge(rs3, o + 1)
                    if o >= 2:
                        act.wait_ge(T0_t, o - 1)
                        act.wait_ge(T0_lo, o - 1)
                    for m in range(OCT):
                        last = nc.scalar.activation(T0[:, o % 2, m, :], outacc[:, o * OCT + m, :], ACT.Relu,
                                                    bias=nmr[:, 1, o % 2, m:m + 1], scale=rs[:, 1, o % 2, m:m + 1])
                    last.then_inc(T0_ready, 1)
                    act.wait_ge(T0_ready, o + 1)
                    nc.scalar.activation(vw_hi[:, o * OCT:(o + 1) * OCT, 0:D], T0[:, o % 2, :, :],
                                         ACT.Copy).then_inc(T0_hi, 1)
                o = step - 4
                if 0 <= o < NO:
                    act.wait_ge(T0_t, o + 1)
                    if o:
                        act.wait_ge(T0_w, o)
                    nc.scalar.activation(hT[:, :], acc[0:D, :, :].rearrange("p a b -> p (a b)"),
                                         ACT.Copy).then_inc(T0_tc, 1)

            def copy_acc(strips):
                act.wait_ge(strip_used, strips)
                nc.scalar.activation(accS[:, :], acc[:, 0, :], ACT.Copy).then_inc(acc_copied, 1)

            def event_b(row):
                rows = bass.ds(row * TB, TB)
                act.wait_ge(fin_ready, row + 1)
                nc.scalar.activation(vw_hi[:, rows, D:P], fin4[:, :, 0:D], ACT.Copy).then_inc(rows_hi, 1)
                nc.scalar.activation(part[:, rows, :], fin4[:, :, 2 * D:3 * D], ACT.Copy).then_inc(fin_a, 1)

            def event_c(r):
                rows = bass.ds((NB - 1) * TB - r * TB, TB)
                act.wait_ge(t2_ready, r + 1)
                nc.scalar.activation(uw_hi[:, rows, 0:D], t2[:, :, :], ACT.Copy).then_inc(rows_hi, 1)

            def rest_of_row(base, chunks):
                with act.Fori(1, chunks) as c:
                    for k in range(4):
                        hi_strip(base + c * 4 + (4 + k), k)

            def first_of_row(base, event):
                copy_acc(base)
                event()
                for k in range(4):
                    hi_strip(base + (4 + k), k)

            for k in range(4):
                hi_strip(S_B + k, k)
            with act.Fori(0, NB) as c:
                for k in range(4):
                    hi_strip(c * 4 + (S_B + 4 + k), k)
            with act.Fori(1, NB) as r:
                base = act.snap(r * (4 * NB) + S_B)
                first_of_row(base, lambda: event_b(r - 1))
                rest_of_row(base, NB)
            first_of_row(S_C, lambda: event_b(NB - 1))
            act.wait_ge(uw_zeroed, 2)
            with act.Fori(1, NB) as r:
                base = act.snap(r * (r + 1) * 2 + S_C)
                first_of_row(base, lambda: event_c(r - 1))
                rest_of_row(base, r + 1)
            first_of_row(S_D, lambda: event_c(NB - 1))
            with act.Fori(1, NB - 1) as r:
                base = act.snap(r * (r + 1) * 2 + S_D)
                act.wait_ge(fin_ready, r + (2 * NB - 1))
                first_of_row(base, lambda: None)
                rest_of_row(base, r + 1)
            last_base = S_D + NB * (NB - 1) * 2
            act.wait_ge(fin_ready, 3 * NB - 2)
            first_of_row(last_base, lambda: None)
            with act.Fori(1, NB - 1) as c:
                for k in range(4):
                    hi_strip(c * 4 + (last_base + 4 + k), k)
            act.wait_ge(fin_ready, 3 * NB - 1)
            copy_acc(S_END)

        @block.vector
        def _(dve):
            link_at = [0]

            def link(ins):
                link_at[0] += 1
                ins.then_inc(dchain, 1)
                dve.wait_ge(dchain, link_at[0])

            def statistics(src, which, b, done):
                for m in range(OCT):
                    last = nc.vector.bn_stats(stats[:, which, b, m, :], src(m))
                link(last)
                for m in range(OCT):
                    last = nc.vector.bn_aggr(mv[:, which, b, m, :], stats[:, which, b, m, :])
                last.then_inc(done, 1)

            def scales(which, b, done):
                link(nc.vector.reciprocal(rs[:, which, b, :], std[:, which, b, :]))
                nc.vector.scalar_tensor_tensor(out=nmr[:, which, b, :], in0=mv[:, which, b, :, 0], scalar=-1.0,
                                               in1=rs[:, which, b, :], op0=ALU.mult, op1=ALU.mult).then_inc(done, 1)

            dve.wait_ge(par_in, 16 * 7)
            link(nc.vector.tensor_tensor(par_p[:, :], par[:, :, 0], par[:, :, 1], ALU.mult))
            dve.wait_ge(pd_t, 1)
            nu = NU // P
            nc.vector.tensor_scalar(pd[:, 0:nu], psT[:, 0, 0:nu], par_p[:, 0:1], None, ALU.mult).then_inc(pd_ready, 1)
            nc.vector.tensor_scalar(pd[:, nu:NT], psT[:, 0, nu:NT], par_p[:, 1:2], None, ALU.mult).then_inc(pd_ready, 1)
            dve.wait_ge(pd_ready, 2)
            dve.wait_ge(x_in, 16)
            for step in range(NO + 4):
                o = step
                if o < NO:
                    if o >= 2:
                        dve.wait_ge(std1, o - 1)
                    statistics(lambda m: xin[:, o * OCT + m, :], 0, o % 2, mean1)
                o = step - 1
                if 0 <= o < NO:
                    dve.wait_ge(std1, o + 1)
                    if o >= 2:
                        dve.wait_ge(h0_ready, o - 1)
                    scales(0, o % 2, rs1)
                o = step - 3
                if 0 <= o < NO:
                    dve.wait_ge(h0_w, o + 1)
                    w = fin[:, o % 2 * RB:(o % 2 + 1) * RB].rearrange("p (m d) -> p m d", d=D)
                    tiles = slice(o * OCT, (o + 1) * OCT)
                    link(nc.vector.tensor_tensor(tmp[:, :, :], w,
                                                 pd[:, tiles].unsqueeze(2).to_broadcast([P, OCT, D]), ALU.mult))
                    nc.vector.tensor_tensor(evec[:, tiles, :], tmp[:, :, :], h0[:, tiles, :],
                                            ALU.add).then_inc(e_ready, 1)
                    dve.wait_ge(e_ready, o + 1)

            def lo_strip(s, k):
                dve.wait_ge(hi_ready, s + 1)
                nc.vector.tensor_tensor(lo[:, k, :], psT[:, k, :], f32(hi[:, k, :]), ALU.subtract).then_inc(lo_ready, 1)

            tp = fin[:, :].rearrange("p (j c) -> p j c", j=2)

            def t_low(j, b):
                dve.wait_ge(t_hi, j)
                nc.vector.tensor_tensor(tT[:, b, :, D:P], tp[:, :, 0:D], f32(tT[:, b, :, 0:D]),
                                        ALU.subtract).then_inc(t_split, 1)

            def add_group(j, g, b):
                dve.wait_ge(acc_free, j * 10 + 2)
                dve.wait_ge(strip_used, j * SA + g * 2 + 2)
                rows = bass.ds(g * RB, RB)
                nc.vector.tensor_tensor(hacc[:, rows], acc[:, b, :], hacc[:, rows], ALU.add).then_inc(acc_free, 1)

            t_low(1, 0)
            for k in range(4):
                lo_strip(k, k)
            dve.wait_ge(acc_free, 2)

            def block_a(j, b, final=False):
                with dve.Fori(0, CA - 1) as c:
                    for k in range(4):
                        lo_strip(j * SA + c * 4 + 4 + k, k)
                        if k % 2:
                            add_group(j, c * 2 + k // 2, k // 2)
                if not final:
                    t_low(j + 2, 1 - b)
                for k in range(4):
                    if not final:
                        lo_strip(j * SA + SA + k, k)
                    if k % 2:
                        add_group(j, 2 * (CA - 1) + k // 2, k // 2)

            with dve.Fori(0, NJ // 2 - 1) as it:
                block_a(it * 2, 0)
                block_a(it * 2 + 1, 1)
            block_a(NJ - 2, 0)
            block_a(NJ - 1, 1, final=True)

            dve.wait_ge(xr_ready, 1)
            for step in range(NO + 6):
                o = step
                if o < NO:
                    dve.wait_ge(h_row, o + 1)
                    if o >= 2:
                        dve.wait_ge(std2, o - 1)
                    statistics(lambda m: psT[:, o % 4, m * D:(m + 1) * D], 0, o % 2, mean2)
                o = step - 1
                if 0 <= o < NO:
                    dve.wait_ge(std2, o + 1)
                    if o >= 2:
                        dve.wait_ge(hn_ready, o - 1)
                    scales(0, o % 2, rs2)
                o = step - 2
                if 0 <= o < NO:
                    tiles = slice(o * OCT, (o + 1) * OCT)
                    dve.wait_ge(hn_ready, o + 1)
                    link(nc.vector.tensor_tensor(tmp[:, :, :], tmp[:, :, :],
                                                 vecs[:, 0:1, :].to_broadcast([P, OCT, D]), ALU.mult))
                    link(nc.vector.tensor_tensor(outacc[:, tiles, :], tmp[:, :, :], part[:, tiles, :], ALU.add))
                    if o >= 2:
                        dve.wait_ge(std3, o - 1)
                    statistics(lambda m: outacc[:, o * OCT + m, :], 1, o % 2, x1_ready)
                o = step - 3
                if 0 <= o < NO:
                    dve.wait_ge(std3, o + 1)
                    if o >= 2:
                        dve.wait_ge(T0_ready, o - 1)
                    scales(1, o % 2, rs3)
                o = step - 4
                if 0 <= o < NO:
                    tiles = slice(o * OCT, (o + 1) * OCT)
                    dve.wait_ge(T0_hi, o + 1)
                    nc.vector.tensor_tensor(vw_lo[:, tiles, 0:D], T0[:, o % 2, :, :], f32(vw_hi[:, tiles, 0:D]),
                                            ALU.subtract).then_inc(T0_lo, 1)
                    link(nc.vector.tensor_tensor(outacc[:, tiles, :], outacc[:, tiles, :],
                                                 vecs[:, 2:3, :].to_broadcast([P, OCT, D]), ALU.add))
                o = step - 5
                if 0 <= o < NO:
                    tiles = slice(o * OCT, (o + 1) * OCT)
                    dve.wait_ge(T0_w, o + 1)
                    w = fin[:, o % 2 * RB:(o % 2 + 1) * RB].rearrange("p (m d) -> p m d", d=D)
                    nc.vector.tensor_tensor(outacc[:, tiles, :], w, outacc[:, tiles, :], ALU.add).then_inc(T0_out, 1)
            dve.wait_ge(T0_out, NO)

            def event_b(row):
                rows = bass.ds(row * TB, TB)
                dve.wait_ge(fin_a, row + 1)
                nc.vector.tensor_tensor(vw_lo[:, rows, D:P], fin4[:, :, 0:D], f32(vw_hi[:, rows, D:P]),
                                        ALU.subtract).then_inc(rows_ready, 1)
                nc.vector.tensor_tensor(outacc[:, rows, :], fin4[:, :, D:2 * D], outacc[:, rows, :],
                                        ALU.add).then_inc(fin_v, 1)

            def event_c(r):
                rows = bass.ds((NB - 1) * TB - r * TB, TB)
                dve.wait_ge(fin_ready, r + (NB + 1))
                dve.wait_ge(fin_a, NB)
                dve.wait_ge(rows_ready, r + NB)
                nc.vector.tensor_tensor(t2[:, :, :], fin4[:, :, 0:D], part[:, rows, :], ALU.add).then_inc(dchain, 1)
                dve.wait_ge(dchain, r * 2 + (link_at[0] + 1))
                nc.vector.scalar_tensor_tensor(out=t2[:, :, :], in0=t2[:, :, :], scalar=2.0,
                                               in1=f32(vw_hi[:, rows, 0:D]),
                                               op0=ALU.mult, op1=ALU.subtract).then_inc(dchain, 1)
                dve.wait_ge(dchain, r * 2 + (link_at[0] + 2))
                nc.vector.tensor_tensor(t2[:, :, :], t2[:, :, :], f32(vw_lo[:, rows, 0:D]),
                                        ALU.subtract).then_inc(t2_ready, 1)
                nc.vector.tensor_tensor(outacc[:, rows, :], fin4[:, :, D:2 * D], outacc[:, rows, :],
                                        ALU.add).then_inc(fin_v, 1)
                dve.wait_ge(rows_hi, r + (NB + 1))
                nc.vector.tensor_tensor(uw_lo[:, rows, 0:D], t2[:, :, :], f32(uw_hi[:, rows, 0:D]),
                                        ALU.subtract).then_inc(rows_ready, 1)

            def event_d(r):
                rows = bass.ds(r * TB, TB)
                dve.wait_ge(fin_ready, r + (2 * NB + 1))
                nc.vector.tensor_tensor(outacc[:, rows, :], fin4[:, :, 0:D], outacc[:, rows, :],
                                        ALU.add).then_inc(out_ready, 1)

            def first_of_row(base, event):
                event()
                for k in range(4):
                    lo_strip(base + (4 + k), k)

            def rest_of_row(base, chunks):
                with dve.Fori(1, chunks) as c:
                    for k in range(4):
                        lo_strip(base + c * 4 + (4 + k), k)

            for k in range(4):
                lo_strip(S_B + k, k)
            with dve.Fori(0, NB) as c:
                for k in range(4):
                    lo_strip(c * 4 + (S_B + 4 + k), k)
            with dve.Fori(1, NB) as r:
                base = dve.snap(r * (4 * NB) + S_B)
                first_of_row(base, lambda: event_b(r - 1))
                rest_of_row(base, NB)
            first_of_row(S_C, lambda: event_b(NB - 1))
            dve.wait_ge(fin_v, NB)
            with dve.Fori(1, NB) as r:
                base = dve.snap(r * (r + 1) * 2 + S_C)
                first_of_row(base, lambda: event_c(r - 1))
                rest_of_row(base, r + 1)
            first_of_row(S_D, lambda: event_c(NB - 1))
            dve.wait_ge(fin_v, 2 * NB)
            with dve.Fori(1, NB - 1) as r:
                base = dve.snap(r * (r + 1) * 2 + S_D)
                first_of_row(base, lambda: event_d(r - 1))
                rest_of_row(base, r + 1)
            last_base = S_D + NB * (NB - 1) * 2
            first_of_row(last_base, lambda: event_d(NB - 2))
            with dve.Fori(1, NB - 1) as c:
                for k in range(4):
                    lo_strip(c * 4 + (last_base + 4 + k), k)
            event_d(NB - 1)

        @block.tensor
        def _(pe):
            mm = nc.tensor.matmul
            pe.wait_ge(const_ready, 2)
            pe.wait_ge(par_in, 16 * 7)
            nc.tensor.transpose(psT[:, 0, 0:NT], dg_row[:, :], ident[0:NT, 0:NT]).then_inc(pd_t, 1)

            def turn(src, done):
                for m in range(OCT):
                    last = nc.tensor.transpose(acc[0:D, m // 4, m % 4 * P:(m % 4 + 1) * P], src[:, m, :],
                                               ident[:, :])
                last.then_inc(done, 1)

            def times(w, o, done):
                for m in range(OCT):
                    at = o % 2 * RB + m * D
                    last = mm(fin[:, at:at + D], hT[:, m * P:(m + 1) * P], w, start=True, stop=True)
                last.then_inc(done, 1)

            pe.wait_ge(w_in, 64)
            for o in range(NO):
                pe.wait_ge(h0_ready, o + 1)
                if o:
                    pe.wait_ge(h0_tc, o)
                turn(h0[:, o * OCT:(o + 1) * OCT, :], h0_t)
                pe.wait_ge(h0_tc, o + 1)
                if o >= 2:
                    pe.wait_ge(e_ready, o - 1)
                times(w_ui[:, 0 if o * OCT * P < NU else 1, :], o, h0_w)

            def t_product(slot0, rt, level, inc=None):
                if rt % 8 == 0:
                    pe.wait_ge(loaded[slot0 + rt // 8], level)
                for j in range(2):
                    at = (rt % 8) * CW + j * P
                    last = mm(fin[:, j * RB:j * RB + D], nat[:, slot0 + rt // 8, at:at + P], evec[:, rt, :],
                              start=rt == 0, stop=rt == NT - 1)
                    if inc is not None and j == 0:
                        last.then_inc(inc, 1)
                if rt == NT - 1:
                    last.then_inc(t_ready, 1)

            def transpose_a(slot, k):
                for m in range(4):
                    at = ((k // 2) * 4 + m) * CW + (k % 2) * P
                    last = nc.tensor.transpose(psT[:, k, m * P:(m + 1) * P], nat[:, slot, at:at + P], ident[:, :])
                last.then_inc(transposed, 1)

            def block_a(j, b, level, last_block=False):
                slot0, next0 = b * CA, (1 - b) * CA
                for q in range(SA):
                    c, k = q // 4, q % 4
                    if q == 0:
                        pe.wait_ge(t_split, j + 1)
                    pe.wait_ge(lo_ready, j * SA + q + 1)
                    ahead = not (last_block and q >= SA - 4)
                    next_slot = slot0 + c + 1 if c < CA - 1 else next0
                    if ahead:
                        transpose_a(next_slot, k)
                    bank, tile = k // 2, k % 2
                    if tile == 0:
                        pe.wait_ge(acc_free, j * 10 + q // 2 + 1)
                    first = mm(acc[:, bank, :], tT[:, b, tile, :], hi[:, k, :], start=tile == 0, stop=False)
                    if ahead and k == 3:
                        first.then_inc(slot_used[next_slot], 1)
                    mm(acc[:, bank, :], tT[:, b, tile, :], lo[:, k, :], start=False, stop=tile == 1).then_inc(strip_used, 1)
                    if not last_block and q < 16:
                        for rt in range(q * NT // 16, (q + 1) * NT // 16):
                            t_product(next0, rt, level)

            pe.wait_ge(e_ready, NO)
            for rt in range(8):
                t_product(0, rt, 16)
            for k in range(4):
                transpose_a(0, k)
            for rt in range(8, NT):
                t_product(0, rt, 16, slot_used[0] if rt == 8 else None)
            with pe.Fori(0, NJ // 2 - 1) as it:
                block_a(it * 2, 0, it * 16 + 16)
                block_a(it * 2 + 1, 1, it * 16 + 32)
            block_a(NJ - 2, 0, NJ // 2 * 16)
            block_a(NJ - 1, 1, None, last_block=True)

            pe.wait_ge(acc_free, 10 * NJ + 2)
            pe.wait_ge(consts, 11)
            for step in range(NO + 4):
                o = step
                if o < NO:
                    if o >= 4:
                        pe.wait_ge(hn_ready, o - 3)
                    for m in range(OCT):
                        last = mm(psT[:, o % 4, m * D:(m + 1) * D], hacc[:, (o * OCT + m) * P:(o * OCT + m + 1) * P],
                                  r_sum[:, :], start=True, stop=True)
                    last.then_inc(h_row, 1)
                o = step - 4
                if 0 <= o < NO:
                    pe.wait_ge(T0_ready, o + 1)
                    if o:
                        pe.wait_ge(T0_tc, o)
                    turn(T0[:, o % 2, :, :], T0_t)
                    pe.wait_ge(T0_tc, o + 1)
                    if o >= 2:
                        pe.wait_ge(T0_out, o - 1)
                    times(w_0[:, :], o, T0_w)

            def transpose_b(slot, k, level=None):
                if level is not None:
                    pe.wait_ge(loaded[slot], level)
                for m in range(TB):
                    at = m * RB + k * P
                    last = nc.tensor.transpose(psT[:, k, m * P:(m + 1) * P], nat[:, slot, at:at + P], ident[:, :])
                last.then_inc(transposed, 1)

            def products(phase, j, k, start, stop, leaves=()):
                n = TB * j + k
                if phase == "B":
                    terms = [(vw_hi, hi), (vw_lo, hi), (vw_hi, lo)]
                elif phase == "C":
                    terms = [(uw_hi, hi), (uw_lo, hi), (uw_hi, lo)]
                else:
                    terms = [(vw_hi, hi), (vw_hi, lo)]
                for i, (v, a) in enumerate(terms):
                    last = mm(acc[:, 0, :], v[:, n, :], a[:, k, :], start=start and i == 0,
                              stop=stop and i == len(terms) - 1)
                    if i == 0 and leaves:
                        last.then_inc(leaves[0], 1)
                last.then_inc(strip_used, 1)

            def finish(row, rhs):
                pe.wait_ge(acc_copied, row + 1)
                for m in range(TB):
                    last = mm(fin4[:, m, 0:rhs.shape[1]], accS[:, m * P:(m + 1) * P], rhs[:, :], start=True, stop=True)
                last.then_inc(fin_ready, 1)

            def chunk(phase, j, base, n, ahead, level, first=False, last=False, close=None, prior=None):
                def t(k):
                    if ahead is not None:
                        pe.wait_ge(lo_ready, base + (4 * n + k + 1))
                        transpose_b(ahead, k, level if k == 0 else None)

                def p(k):
                    if ahead is None:
                        pe.wait_ge(lo_ready, base + (4 * n + k + 1))
                    leaves = ()
                    if k == 3 and ahead is not None:
                        leaves = (slot_used[ahead],)
                    if k == 0 and prior is not None:
                        leaves = (slot_used[prior],)
                    products(phase, j, k, first and k == 0, last and k == 3, leaves)

                t(0)
                if close is not None:
                    t(1)
                    close()
                    p(0)
                    p(1)
                    rest = (2, 3)
                else:
                    p(0)
                    rest = (1, 2, 3)
                for k in rest:
                    t(k)
                    p(k)

            def level_b(r):
                return r * 16 + 16 * (NB + 1)

            pe.wait_ge(T0_lo, NO)
            pe.wait_ge(T0_out, NO)
            pe.wait_ge(T0_hi, NO)
            for k in range(4):
                transpose_b(NB - 1, k, level_b(0) if k == 0 else None)

            def row_b(r, base, **head):
                chunk("B", NB - 1, base, 0, NB - 2, level_b(r), first=True, **head)
                for j in reversed(range(1, NB - 1)):
                    if j == NB - 2 and "close" in head:
                        pe.wait_ge(rows_ready, r)
                        pe.wait_ge(fin_v, r)
                    chunk("B", j, base, NB - 1 - j, j - 1, level_b(r))
                chunk("B", 0, base, NB - 1, NB - 1, level_b(r + 1), last=True)

            row_b(0, S_B, prior=NB - 1)
            with pe.Fori(1, NB) as r:
                row_b(r, pe.snap(r * (4 * NB) + S_B), close=lambda: finish(r - 1, r_B))

            def level_c(j, r):
                return r * 16 + 16 * (NB + 2 + j)

            def close_c(r):
                pe.wait_ge(fin_v, r + (NB - 1))
                pe.wait_ge(fin_a, NB)
                finish(r + (NB - 1), r_C)
                pe.wait_ge(rows_ready, NB + 1)

            def close_last_b():
                finish(NB - 1, r_B)
                pe.wait_ge(uw_ready, 2 * NB)

            chunk("C", NB - 1, S_C, 0, NB - 1, level_c(NB - 1, 1), first=True, last=True, close=close_last_b)
            with pe.Fori(1, NB - 1) as r:
                base = pe.snap(r * (r + 1) * 2 + S_C)
                chunk("C", NB - 1, base, 0, NB - 2, level_c(NB - 2, r), first=True, close=lambda: close_c(r))
                for j in reversed(range(1, NB - 1)):
                    with pe.If(r > NB - 1 - j):
                        pe.wait_ge(rows_ready, 2 * NB - j)
                        chunk("C", j, base, NB - 1 - j, j - 1, level_c(j - 1, r))
                    pe.end_ifs()
                    with pe.If(r == NB - 1 - j):
                        chunk("C", j, base, NB - 1 - j, NB - 1, level_c(NB - 1, r + 1), last=True)
                    pe.end_ifs()
            end = NB - 1
            base_end = S_C + end * (end + 1) * 2
            chunk("C", NB - 1, base_end, 0, NB - 2, level_c(NB - 2, end), first=True, close=lambda: close_c(end))
            for j in reversed(range(1, NB - 1)):
                pe.wait_ge(rows_ready, 2 * NB - j)
                chunk("C", j, base_end, NB - 1 - j, j - 1, level_c(j - 1, end))

            def level_d(r):
                return r * 16 + 16 * (2 * NB + 2)

            chunk("C", 0, base_end, NB - 1, 0, level_d(0), last=True)

            def close_last_c():
                pe.wait_ge(fin_v, 2 * NB - 1)
                finish(2 * NB - 1, r_C)
                pe.wait_ge(t2_copied, 2 * NB)

            def close_d(r):
                finish(r + (2 * NB - 1), r_D)

            chunk("D", 0, S_D, 0, 0, level_d(1), first=True, last=True, close=close_last_c)
            pe.wait_ge(fin_v, 2 * NB)
            with pe.Fori(1, NB - 1) as r:
                base = pe.snap(r * (r + 1) * 2 + S_D)
                chunk("D", 0, base, 0, 1, level_d(r), first=True, close=lambda: close_d(r))
                for j in range(1, NB - 1):
                    with pe.If(r > j):
                        chunk("D", j, base, j, j + 1, level_d(r))
                    pe.end_ifs()
                    with pe.If(r == j):
                        chunk("D", j, base, j, 0, level_d(r + 1), last=True)
                    pe.end_ifs()
                pe.wait_ge(out_ready, r)
            base_end = S_D + end * (end + 1) * 2
            chunk("D", 0, base_end, 0, 1, level_d(end), first=True, close=lambda: close_d(end))
            for j in range(1, NB - 1):
                chunk("D", j, base_end, j, j + 1, level_d(end))
            chunk("D", NB - 1, base_end, NB - 1, None, None, last=True)
            pe.wait_ge(out_ready, NB - 1)
            finish(3 * NB - 1, r_D)


_NAMES = ["x", "adj", "L0_gnn_W_u", "L0_gnn_diag_u", "L0_gnn_par_u", "L0_gnn_W_i", "L0_gnn_diag_i", "L0_gnn_par_i",
          "L0_gnn_ln_gamma", "L0_gnn_ln_beta", "L1_gnn_weight", "L1_gnn_bias"]


def kernel(**inputs):
    import numpy as np
    import concourse.bacc as bacc
    from concourse import mybir as mb
    from concourse.bass_utils import run_bass_kernel_spmd as run

    nc = bacc.Bacc("TRN2", target_bir_lowering=False, num_devices=1)
    arrays, args = {}, []
    for name in _NAMES:
        a = np.ascontiguousarray(inputs[name])
        arrays[f"in_{name}"] = a
        args.append(nc.dram_tensor(f"in_{name}", a.shape, mb.dt.from_np(a.dtype), kind="ExternalInput").ap())
    args.append(nc.dram_tensor("result", (N, D), F32, kind="ExternalOutput").ap())
    build(nc, *args)
    r = run(nc, [arrays], core_ids=[0])
    return r.results[0]["result"]
```

```python
import concourse.bass as bass
from concourse import mybir
from contextlib import ExitStack

F32 = mybir.dt.float32
F32R = mybir.dt.float32r
ALU = mybir.AluOpType
ACT = mybir.ActivationFunctionType

P = 128
N = 5120
D = 64
NT = N // P
NU = 2048
RB = 512
NB = N // RB
TB = RB // P
CW = 256
CR = 1024
CA = N // CR
NJ = N // CW
SA = CA * 4
OCT = 8
NO = NT // OCT
EPS = 1e-5
NR = 4
UA = NT // 2
Q_T = 16
Q_NEXT = 17
HEAD = 4
PAIRS = NB // 2


S_B = NJ * SA
S_C = S_B + NB * NB * 4
S_D = S_C + NB * (NB + 1) // 2 * 4
S_END = S_D + NB * (NB + 1) // 2 * 4


def pieces_beside(q):
    first = SA - Q_NEXT
    if q < Q_T:
        share = UA - first
        return [(1, first + n) for n in range(q * share // Q_T, (q + 1) * share // Q_T)]
    return [(2, q - Q_NEXT)] if q >= Q_NEXT else []


def build(nc, x, adj, W_u, diag_u, par_u, W_i, diag_i, par_i, gamma, beta, weight, bias, out):
    ctx = ExitStack()
    with ctx:
        def sb(name, shape, dt=F32):
            return ctx.enter_context(nc.sbuf_tensor(name, shape, dt))

        def pb(name, shape):
            return ctx.enter_context(nc.psum_tensor(name, shape, F32))

        def sem(name):
            return ctx.enter_context(nc.semaphore(name))

        nat = sb("nat", [P, NB, 2048])
        rowwise = ExitStack()
        hT = rowwise.enter_context(nc.sbuf_tensor("hT", [D, OCT * P], F32))
        tmp = rowwise.enter_context(nc.sbuf_tensor("tmp", [P, OCT, D], F32))
        T0 = rowwise.enter_context(nc.sbuf_tensor("T0", [P, 2, OCT, D], F32))
        stats = rowwise.enter_context(nc.sbuf_tensor("stats", [P, 2, 2, OCT, 6], F32))
        w_ui = rowwise.enter_context(nc.sbuf_tensor("w_ui", [D, 2, D], F32))
        dg_row = rowwise.enter_context(nc.sbuf_tensor("dg_row", [NT, P], F32))
        rowwise.close()
        hi = sb("hi", [P, 4, RB], F32R)
        lo = sb("lo", [P, 4, RB], F32R)
        phase_a = ExitStack()
        e_hl = phase_a.enter_context(nc.sbuf_tensor("e_hl", [P, NT, P], F32R))
        n_hi = phase_a.enter_context(nc.sbuf_tensor("n_hi", [P, NR, 2 * CW], F32R))
        n_lo = phase_a.enter_context(nc.sbuf_tensor("n_lo", [P, NR, 2 * CW], F32R))
        tS = phase_a.enter_context(nc.sbuf_tensor("tS", [P, CW], F32))
        phase_a.close()
        vw_hi = sb("vw_hi", [P, NT, P], F32R)
        vw_lo = sb("vw_lo", [P, NT, P], F32R)
        outacc = sb("outacc", [P, NT, D])
        part = sb("part", [P, NT, D])
        ident = sb("ident", [P, P])
        r_sum = sb("r_sum", [P, D])
        r_B = sb("r_B", [P, 3 * D])
        r_C = sb("r_C", [P, 2 * D])
        r_D = sb("r_D", [P, D])
        w_0 = sb("w_0", [D, D])
        wk = sb("wk", [P, 4, D])
        vecs = sb("vecs", [P, 3, D])
        par = sb("par", [P, 2, 2])
        pd = sb("pd", [P, NT])
        par_p = sb("par_p", [P, 2])
        eps = sb("eps", [P, 1])
        tT = sb("tT", [P, 2, 2, P], F32R)
        accS = sb("accS", [P, RB])
        mv = sb("mv", [P, 2, 2, OCT, 2])
        rs = sb("rs", [P, 2, 2, OCT])
        nmr = sb("nmr", [P, 2, 2, OCT])
        std = sb("std", [P, 2, 2, OCT])
        t2 = sb("t2", [P, TB, D])
        early = ExitStack()

        hacc = early.enter_context(nc.sbuf_tensor("hacc", [P, N], F32))
        evec = early.enter_context(nc.sbuf_tensor("evec", [P, NT, D], F32))
        h0 = early.enter_context(nc.sbuf_tensor("h0", [P, NT, D], F32))
        early.close()
        uw_hi = sb("uw_hi", [P, NT, P], F32R)
        uw_lo = sb("uw_lo", [P, NT, P], F32R)
        xin = outacc

        psT = pb("psT", [P, 4, RB])
        acc = pb("acc", [P, 2, RB])
        fin = pb("fin", [P, 2 * RB])

        loaded = [sem(f"loaded{s}") for s in range(NB)]
        slot_used = [sem(f"slot_used{s}") for s in range(NB)]
        x_in, par_in, w_in = sem("x_in"), sem("par_in"), sem("w_in")
        const_ready, consts = sem("const_ready"), sem("consts")
        pd_t, pd_ready = sem("pd_t"), sem("pd_ready")
        dchain, pchain = sem("dchain"), sem("pchain")
        transposed, hi_ready, lo_ready, strip_used = (
            sem("transposed"), sem("hi_ready"), sem("lo_ready"), sem("strip_used"))
        n_hi_ready, n_lo_ready, n_used = sem("n_hi_ready"), sem("n_lo_ready"), sem("n_used")
        t_ready, t_copied, t_row, t_hi, t_split = (sem(n) for n in ("t_ready", "t_copied", "t_row", "t_hi", "t_split"))
        e_hi, e_split = sem("e_hi"), sem("e_split")
        acc_free = sem("acc_free")
        mean1, std1, rs1, h0_ready, h0_t, h0_tc, h0_w, e_ready = (sem(n) for n in (
            "mean1", "std1", "rs1", "h0_ready", "h0_t", "h0_tc", "h0_w", "e_ready"))
        xr_ready = sem("xr_ready")
        h_row, mean2, std2, rs2, hn_ready, x1_ready, std3, rs3, T0_ready, T0_hi, T0_t, T0_tc, T0_w, T0_lo, T0_out = (
            sem(n) for n in ("h_row", "mean2", "std2", "rs2", "hn_ready", "x1_ready", "std3", "rs3", "T0_ready",
                             "T0_hi", "T0_t", "T0_tc", "T0_w", "T0_lo", "T0_out"))
        uw_zeroed, vw_zeroed = sem("uw_zeroed"), sem("vw_zeroed")
        acc_copied, fin_ready, fin_a, fin_v, rows_hi, rows_ready, uw_ready, t2_ready, t2_copied = (sem(n) for n in (
            "acc_copied", "fin_ready", "fin_a", "fin_v", "rows_hi", "rows_ready", "uw_ready", "t2_ready",
            "t2_copied"))
        out_ready, out_sent = sem("out_ready"), sem("out_sent")

        def f32(ap):
            return ap.bitcast(F32)

        fin4 = fin[:, :].rearrange("p (m c) -> p m c", m=TB)
        t_rows = fin[:, RB:RB + 2 * D].rearrange("p (j d) -> p j d", j=2)
        out_v = out.rearrange("(t p) d -> p t d", p=P)
        x_v = x.rearrange("(t p) d -> p t d", p=P)

        def used_before_d(slot):
            return 2 * NB + 1 + min(NB - HEAD, slot + 1)

        block = ctx.enter_context(nc.Block())

        @block.sync
        def _(sp):
            sp.dma_start(xin[:, :, :], x_v).then_inc(x_in, 16)
            sp.dma_start(w_ui[:, 0, :], W_u).then_inc(w_in, 16)
            sp.dma_start(w_ui[:, 1, :], W_i).then_inc(w_in, 16)
            sp.dma_start(wk[0:D, :, :], weight.rearrange("k i o -> i k o")).then_inc(w_in, 16)
            sp.dma_start(wk[D:P, :, :], weight.rearrange("k i o -> i k o")).then_inc(w_in, 16)
            adj_a = adj.rearrange("(c m p) n -> c p m n", p=P, m=CR // P)
            adj_b = adj.rearrange("(i m p) n -> i p m n", p=P, m=TB)

            def slot_left(slot, uses):
                if not isinstance(uses, int):
                    sp.lower_val(uses)
                sp.wait_ge(w_in, 64)
                sp.wait_ge(slot_used[slot], uses)

            def load_a(slot, c, col, uses=None):
                dst = nat[:, slot, :].rearrange("p (m n) -> p m n", n=CW)
                src = adj_a[c, :, :, bass.ds(col, CW)]
                if uses is not None:
                    slot_left(slot, uses)
                sp.dma_start(dst, src).then_inc(loaded[slot], 16)

            def load_b(j, row, uses, slot=None):
                slot = j if slot is None else slot
                dst = nat[:, slot, :].rearrange("p (m n) -> p m n", n=RB)
                src = adj[bass.ds(row, RB), j * RB:(j + 1) * RB].rearrange("(m p) n -> p m n", p=P)
                slot_left(slot, uses)
                sp.dma_start(dst, src).then_inc(loaded[slot], 16)

            for slot in range(NB):
                load_a(slot, slot % CA, slot // CA * CW)
            with sp.Fori(1, NJ // 2) as it:
                for slot in range(NB):
                    load_a(slot, slot % CA, it * (2 * CW) + slot // CA * CW, it)
            with sp.Fori(0, NB) as r:
                for j in reversed(range(NB)):
                    load_b(j, r * RB, r + NB)
            slot = NB
            for r in range(HEAD):
                for j in reversed(range(NB - 1 - r, NB)):
                    slot -= 1
                    load_b(j, (NB - 1 - r) * RB, 2 * NB, slot)
            with sp.Fori(HEAD, NB) as r:
                row = (NB - 1) * RB - r * RB
                for j in reversed(range(NB)):
                    if j >= NB - 1 - HEAD:
                        load_b(j, row, r + (2 * NB + 1 - HEAD))
                    else:
                        with sp.If(r > NB - 2 - j):
                            load_b(j, row, r + (NB + 2 + j))
                        sp.end_ifs()
            with sp.Fori(0, PAIRS) as m:
                for j in range(NB):
                    if j <= PAIRS:
                        load_b(j, (NB - 1) * RB - m * RB, m + used_before_d(NB - 1 - j), NB - 1 - j)
                    else:
                        with sp.If(m < NB - j):
                            load_b(j, (NB - 1) * RB - m * RB, m + used_before_d(NB - 1 - j), NB - 1 - j)
                        sp.end_ifs()
                for j in range(PAIRS):
                    if j == 0:
                        load_b(j, m * RB, m + (used_before_d(j) + 1), j)
                    else:
                        with sp.If(m > j - 1):
                            load_b(j, m * RB, m + (used_before_d(j) + 1), j)
                        sp.end_ifs()

        @block.gpsimd
        def _(pool):
            nc.gpsimd.memset(ident[:, :], 0.0).then_inc(pchain, 1)
            nc.gpsimd.memset(eps[:, :], EPS).then_inc(const_ready, 1)
            pool.wait_ge(pchain, 1)
            nc.gpsimd.affine_select(out=ident[:, :], in_=ident[:, :], compare_op=ALU.not_equal, fill=1.0, base=0,
                                    pattern=[[-1, P]], channel_multiplier=1).then_inc(const_ready, 1)
            nc.gpsimd.memset(hacc[:, 0:N // 2], 0.0).then_inc(acc_free, 1)
            nc.gpsimd.memset(hacc[:, N // 2:N], 0.0).then_inc(acc_free, 1)
            nc.gpsimd.memset(r_B[:, :], 0.0).then_inc(pchain, 1)
            nc.gpsimd.memset(r_C[:, :], 0.0).then_inc(pchain, 1)
            pool.wait_ge(const_ready, 2)
            pool.wait_ge(pchain, 3)
            pool.wait_ge(w_in, 64)
            for h in (slice(0, D), slice(D, P)):
                nc.gpsimd.tensor_copy(r_sum[h, :], ident[h, h]).then_inc(consts, 1)
            nc.gpsimd.tensor_copy(r_B[0:D, 0:D], ident[0:D, 0:D]).then_inc(consts, 1)
            nc.gpsimd.tensor_copy(r_B[D:P, 2 * D:3 * D], ident[D:P, D:P]).then_inc(consts, 1)
            nc.gpsimd.tensor_copy(r_C[D:P, 0:D], ident[D:P, D:P]).then_inc(consts, 1)
            nc.gpsimd.tensor_tensor(r_B[0:D, D:2 * D], wk[0:D, 1, :], wk[0:D, 3, :], ALU.subtract).then_inc(consts, 1)
            nc.gpsimd.tensor_tensor(w_0[:, :], wk[0:D, 0, :], wk[0:D, 2, :], ALU.subtract).then_inc(consts, 1)
            nc.gpsimd.tensor_tensor(r_B[D:P, D:2 * D], wk[D:P, 2, :], wk[D:P, 2, :], ALU.add).then_inc(consts, 1)
            nc.gpsimd.tensor_tensor(r_C[D:P, D:2 * D], wk[D:P, 2, :], wk[D:P, 2, :], ALU.add).then_inc(consts, 1)
            nc.gpsimd.tensor_tensor(r_C[0:D, D:2 * D], wk[0:D, 3, :], wk[0:D, 3, :], ALU.add).then_inc(consts, 1)
            pool.wait_ge(consts, 10)
            nc.gpsimd.tensor_tensor(r_D[:, :], wk[:, 3, :], wk[:, 3, :], ALU.add).then_inc(consts, 1)
            pool.wait_ge(x_in, 16)
            pool.wait_ge(par_in, 16 * 7)
            pool.wait_ge(h0_ready, NO)

            def n_low(u, slot, m):
                pool.wait_ge(n_hi_ready, u + 1)
                nc.gpsimd.tensor_tensor(n_lo[:, m, :].unsqueeze(1), nat[:, slot, m * 2 * CW:(m + 1) * 2 * CW],
                                        f32(n_hi[:, m, :]).unsqueeze(1), ALU.subtract).then_inc(n_lo_ready, 1)

            for c in range(CA):
                for m in range(NR):
                    n_low(c * NR + m, slice(c, c + 1), m)
            for tiles in (slice(0, NT // 2), slice(NT // 2, NT)):
                nc.gpsimd.tensor_tensor(part[:, tiles, :], xin[:, tiles, :], h0[:, tiles, :], ALU.add).then_inc(pchain, 1)
            with pool.Fori(0, NJ // 2 - 1) as it:
                for b in (1, 0):
                    with pool.Fori(0, CA) as c:
                        for m in range(NR):
                            n_low(it * (2 * UA) + c * NR + ((2 - b) * UA + m), bass.ds(c + b * CA, 1), m)
            with pool.Fori(0, CA) as c:
                for m in range(NR):
                    n_low(c * NR + ((NJ - 1) * UA + m), bass.ds(c + CA, 1), m)
            pool.wait_ge(pchain, 5)
            nc.gpsimd.tensor_tensor(part[:, :, :], part[:, :, :],
                                    vecs[:, 1:2, :].to_broadcast([P, NT, D]), ALU.add).then_inc(xr_ready, 1)
            pool.wait_ge(t_row, NJ)
            nc.gpsimd.memset(f32(vw_hi[:, :, D:P]), 0.0).then_inc(vw_zeroed, 1)
            nc.gpsimd.memset(f32(vw_lo[:, :, D:P]), 0.0).then_inc(vw_zeroed, 1)
            pool.wait_ge(h_row, NO)
            nc.gpsimd.memset(f32(uw_hi[:, :, 0:D]), 0.0).then_inc(uw_zeroed, 1)
            nc.gpsimd.memset(f32(uw_lo[:, :, 0:D]), 0.0).then_inc(uw_zeroed, 1)
            with pool.Fori(0, NB) as r:
                pool.wait_ge(rows_ready, r + 1)
                rows = bass.ds(r * TB, TB)
                nc.gpsimd.tensor_copy(uw_hi[:, rows, D:P], f32(vw_hi[:, rows, D:P])).then_inc(uw_ready, 1)
                nc.gpsimd.tensor_copy(uw_lo[:, rows, D:P], f32(vw_lo[:, rows, D:P])).then_inc(uw_ready, 1)
            with pool.Fori(0, NB) as r:
                pool.wait_ge(rows_ready, r + NB + 1)
                rows = bass.ds((NB - 1) * TB - r * TB, TB)
                nc.gpsimd.tensor_copy(vw_hi[:, rows, 0:D], f32(uw_hi[:, rows, 0:D])).then_inc(t2_copied, 1)
                nc.gpsimd.tensor_copy(vw_hi[:, rows, D:P], f32(uw_lo[:, rows, 0:D])).then_inc(t2_copied, 1)
            with pool.Fori(0, PAIRS) as m:
                for b, row in ((0, m * -1 + (NB - 1)), (1, m)):
                    pool.wait_ge(out_ready, m * 2 + (b + 1))
                    pool.dma_start(out[bass.ds(row * RB, RB), :].rearrange("(m p) d -> p m d", p=P),
                                   outacc[:, bass.ds(row * TB, TB), :]).then_inc(out_sent, 16)
            pool.wait_ge(out_sent, 16 * NB)

        @block.scalar
        def _(act):
            act.dma_start(dg_row[0:NU // P, :], diag_u.rearrange("(t p) -> t p", p=P)).then_inc(par_in, 16)
            act.dma_start(dg_row[NU // P:NT, :], diag_i.rearrange("(t p) -> t p", p=P)).then_inc(par_in, 16)
            for n, v in enumerate((par_u, par_i)):
                act.dma_start(par[:, n, :], v.rearrange("(a n) -> a n", a=1).to_broadcast([P, 2])).then_inc(par_in, 16)
            for n, v in enumerate((gamma, beta, bias)):
                act.dma_start(vecs[:, n, :], v.rearrange("(a n) -> a n", a=1).to_broadcast([P, D])).then_inc(par_in, 16)

            act.wait_ge(const_ready, 2)
            for step in range(NO + 5):
                if step < NO:
                    o, b = step, step % 2
                    act.wait_ge(mean1, o + 1)
                    nc.scalar.activation(std[:, 0, b, :], mv[:, 0, b, :, 1], ACT.Sqrt, bias=eps[:, :]).then_inc(std1, 1)
                o = step - 1
                if 0 <= o < NO:
                    act.wait_ge(rs1, o + 1)
                    for m in range(OCT):
                        last = nc.scalar.activation(h0[:, o * OCT + m, :], xin[:, o * OCT + m, :], ACT.Relu,
                                                    bias=nmr[:, 0, o % 2, m:m + 1], scale=rs[:, 0, o % 2, m:m + 1])
                    last.then_inc(h0_ready, 1)
                o = step - 2
                if 0 <= o < NO:
                    act.wait_ge(h0_t, o + 1)
                    if o:
                        act.wait_ge(h0_w, o)
                    nc.scalar.activation(hT[:, :], acc[0:D, :, :].rearrange("p a b -> p (a b)"),
                                         ACT.Copy).then_inc(h0_tc, 1)
                o = step - 4
                if 0 <= o < NO:
                    tiles = slice(o * OCT, (o + 1) * OCT)
                    act.wait_ge(e_ready, o + 1)
                    nc.scalar.activation(e_hl[:, tiles, 0:D], evec[:, tiles, :], ACT.Copy).then_inc(e_hi, 1)

            def hi_strip(s, k):
                act.wait_ge(transposed, s + 1)
                act.wait_ge(strip_used, s - 3)
                nc.scalar.activation(hi[:, k, :], psT[:, k, :], ACT.Copy).then_inc(hi_ready, 1)

            def n_high(u, slot, m, level=None, wait=True):
                if level is not None:
                    act.wait_ge(loaded[slot], level)
                if wait:
                    act.wait_ge(n_used, u - (NR - 1))
                nc.scalar.activation(n_hi[:, m, :], nat[:, slot, m * 2 * CW:(m + 1) * 2 * CW],
                                     ACT.Copy).then_inc(n_hi_ready, 1)

            def t_copy(j):
                act.wait_ge(t_ready, j)
                nc.scalar.activation(tS[:, :], fin[:, 0:CW], ACT.Copy).then_inc(t_copied, 1)

            def t_high(j, b):
                act.wait_ge(t_row, j)
                nc.scalar.activation(tT[:, b, :, 0:D], t_rows[:, :, :], ACT.Copy).then_inc(t_hi, 1)

            for u in range(UA):
                n_high(u, u // NR, u % NR, 16 if u % NR == 0 else None, wait=u >= NR)
                if u == NR - 1:
                    for k in range(4):
                        act.wait_ge(transposed, k + 1)
                        nc.scalar.activation(hi[:, k, :], psT[:, k, :], ACT.Copy).then_inc(hi_ready, 1)
            for u in range(SA - Q_NEXT):
                n_high(UA + u, CA, u, 16 if u == 0 else None)
            t_copy(1)
            t_high(1, 0)
            for q in (0, 1):
                for _, u in pieces_beside(q):
                    n_high(UA + u, CA + u // NR, u % NR, 16 if u % NR == 0 else None)

            def block_a(j, b, level, after, ahead=True, final=False):
                for q in range(16 if final else SA):
                    if q == Q_T and not final:
                        t_copy(j + 2)
                    if q == Q_NEXT + 1 and not final:
                        t_high(j + 2, 1 - b)
                    wraps = q + 2 >= SA
                    for n, u in () if final else pieces_beside((q + 2) % SA):
                        n += wraps
                        slot0, arrived = ((1 - b) * CA, level) if n == 1 else (b * CA, after)
                        if n == 1 or ahead:
                            n_high((j + n) * UA + u, slot0 + u // NR, u % NR, arrived if u % NR == 0 else None)
                    hi_strip(j * SA + (q + 4), q % 4)

            with act.Fori(0, NJ // 2 - 1) as it:
                block_a(it * 2, 0, it * 16 + 16, it * 16 + 32)
                block_a(it * 2 + 1, 1, it * 16 + 32, it * 16 + 32)
            block_a(NJ - 2, 0, NJ // 2 * 16, None, ahead=False)
            block_a(NJ - 1, 1, None, None, final=True)

            for step in range(NO + 5):
                o, b = step, step % 2
                if o < NO:
                    act.wait_ge(mean2, o + 1)
                    nc.scalar.activation(std[:, 0, b, :], mv[:, 0, b, :, 1], ACT.Sqrt, bias=eps[:, :]).then_inc(std2, 1)
                o = step - 1
                if 0 <= o < NO:
                    act.wait_ge(rs2, o + 1)
                    if o:
                        act.wait_ge(x1_ready, o)
                    for m in range(OCT):
                        last = nc.scalar.activation(tmp[:, m, :], psT[:, o % 4, m * D:(m + 1) * D], ACT.Identity,
                                                    bias=nmr[:, 0, o % 2, m:m + 1], scale=rs[:, 0, o % 2, m:m + 1])
                    last.then_inc(hn_ready, 1)
                o = step - 2
                if 0 <= o < NO:
                    act.wait_ge(x1_ready, o + 1)
                    nc.scalar.activation(std[:, 1, o % 2, :], mv[:, 1, o % 2, :, 1], ACT.Sqrt,
                                         bias=eps[:, :]).then_inc(std3, 1)
                o = step - 3
                if 0 <= o < NO:
                    act.wait_ge(rs3, o + 1)
                    if o >= 2:
                        act.wait_ge(T0_t, o - 1)
                        act.wait_ge(T0_lo, o - 1)
                    for m in range(OCT):
                        last = nc.scalar.activation(T0[:, o % 2, m, :], outacc[:, o * OCT + m, :], ACT.Relu,
                                                    bias=nmr[:, 1, o % 2, m:m + 1], scale=rs[:, 1, o % 2, m:m + 1])
                    last.then_inc(T0_ready, 1)
                    act.wait_ge(T0_ready, o + 1)
                    nc.scalar.activation(vw_hi[:, o * OCT:(o + 1) * OCT, 0:D], T0[:, o % 2, :, :],
                                         ACT.Copy).then_inc(T0_hi, 1)
                o = step - 4
                if 0 <= o < NO:
                    act.wait_ge(T0_t, o + 1)
                    if o:
                        act.wait_ge(T0_w, o)
                    nc.scalar.activation(hT[:, :], acc[0:D, :, :].rearrange("p a b -> p (a b)"),
                                         ACT.Copy).then_inc(T0_tc, 1)

            def copy_acc(strips, bank, row):
                act.wait_ge(strip_used, strips)
                if row is not None:
                    act.wait_ge(fin_ready, row)
                nc.scalar.activation(accS[:, :], acc[:, bank, :], ACT.Copy).then_inc(acc_copied, 1)

            def event_b(row):
                rows = bass.ds(row * TB, TB)
                act.wait_ge(fin_ready, row + 1)
                nc.scalar.activation(vw_hi[:, rows, D:P], fin4[:, :, 0:D], ACT.Copy).then_inc(rows_hi, 1)
                nc.scalar.activation(part[:, rows, :], fin4[:, :, 2 * D:3 * D], ACT.Copy).then_inc(fin_a, 1)

            def event_c(r):
                rows = bass.ds((NB - 1) * TB - r * TB, TB)
                act.wait_ge(t2_ready, r + 1)
                nc.scalar.activation(uw_hi[:, rows, 0:D], t2[:, :, :], ACT.Copy).then_inc(rows_hi, 1)

            def row_of_strips(base, chunks, bank, done, event=None, urgent=False):
                copy_acc(base, bank, done)
                if event is not None and urgent:
                    event()
                for k in range(4):
                    hi_strip(base + (4 + k), k)
                    if k == 1 and event is not None and not urgent:
                        event()
                if not isinstance(chunks, int) or chunks > 1:
                    with act.Fori(1, chunks) as c:
                        for k in range(4):
                            hi_strip(base + c * 4 + (4 + k), k)

            for k in range(4):
                hi_strip(S_B + k, k)
            with act.Fori(0, NB) as c:
                for k in range(4):
                    hi_strip(c * 4 + (S_B + 4 + k), k)
            row_of_strips(S_B + 4 * NB, NB, 0, None, lambda: event_b(0))
            with act.Fori(1, PAIRS) as q:
                for b in (0, 1):
                    base = act.snap(q * (8 * NB) + (S_B + 4 * NB * b))
                    row_of_strips(base, NB, 1 - b, q * 2 + (b - 1), lambda: event_b(q * 2 + (b - 1)))
            row_of_strips(S_C, 1, 1, NB - 1, lambda: event_b(NB - 1), urgent=True)
            act.wait_ge(uw_zeroed, 2)
            for r in range(1, HEAD):
                row_of_strips(S_C + 2 * r * (r + 1), r + 1, 1 - r % 2, NB + r - 1, lambda: event_c(r - 1), urgent=r == 1)
            with act.Fori(HEAD // 2, PAIRS) as q:
                for b in (0, 1):
                    r = q * 2 + b
                    base = act.snap(r * (r + 1) * 2 + S_C)
                    row_of_strips(base, r + 1, 1 - b, r + (NB - 1), lambda: event_c(r - 1))
            row_of_strips(S_D, NB, 1, 2 * NB - 1, lambda: event_c(NB - 1), urgent=True)
            row_of_strips(S_D + 4 * NB, 1, 0, 2 * NB)
            with act.Fori(1, PAIRS - 1) as m:
                base = act.snap(m * (4 * (NB + 1)) + S_D)
                row_of_strips(base, NB - m, 1, m * 2 + (2 * NB - 1))
                base = act.snap(m * (4 * NB) + (S_D + 4 * NB))
                row_of_strips(base, m + 1, 0, m * 2 + 2 * NB)
            end = S_END - 4 * (NB + 1)
            row_of_strips(end, PAIRS + 1, 1, 3 * NB - 3)
            row_of_strips(S_END - 4 * PAIRS, PAIRS - 1, 0, 3 * NB - 2)
            copy_acc(S_END, 1, 3 * NB - 1)

        @block.vector
        def _(dve):
            link_at = [0]

            def link(ins):
                link_at[0] += 1
                ins.then_inc(dchain, 1)
                dve.wait_ge(dchain, link_at[0])

            def statistics(src, which, b, done):
                for m in range(OCT):
                    last = nc.vector.bn_stats(stats[:, which, b, m, :], src(m))
                link(last)
                for m in range(OCT):
                    last = nc.vector.bn_aggr(mv[:, which, b, m, :], stats[:, which, b, m, :])
                last.then_inc(done, 1)

            def scales(which, b, done):
                link(nc.vector.reciprocal(rs[:, which, b, :], std[:, which, b, :]))
                nc.vector.scalar_tensor_tensor(out=nmr[:, which, b, :], in0=mv[:, which, b, :, 0], scalar=-1.0,
                                               in1=rs[:, which, b, :], op0=ALU.mult, op1=ALU.mult).then_inc(done, 1)

            dve.wait_ge(par_in, 16 * 7)
            link(nc.vector.tensor_tensor(par_p[:, :], par[:, :, 0], par[:, :, 1], ALU.mult))
            dve.wait_ge(pd_t, 1)
            nu = NU // P
            nc.vector.tensor_scalar(pd[:, 0:nu], psT[:, 0, 0:nu], par_p[:, 0:1], None, ALU.mult).then_inc(pd_ready, 1)
            nc.vector.tensor_scalar(pd[:, nu:NT], psT[:, 0, nu:NT], par_p[:, 1:2], None, ALU.mult).then_inc(pd_ready, 1)
            dve.wait_ge(pd_ready, 2)
            dve.wait_ge(x_in, 16)
            for step in range(NO + 5):
                o = step
                if o < NO:
                    if o >= 2:
                        dve.wait_ge(std1, o - 1)
                    statistics(lambda m: xin[:, o * OCT + m, :], 0, o % 2, mean1)
                o = step - 1
                if 0 <= o < NO:
                    dve.wait_ge(std1, o + 1)
                    if o >= 2:
                        dve.wait_ge(h0_ready, o - 1)
                    scales(0, o % 2, rs1)
                o = step - 3
                if 0 <= o < NO:
                    dve.wait_ge(h0_w, o + 1)
                    w = fin[:, o % 2 * RB:(o % 2 + 1) * RB].rearrange("p (m d) -> p m d", d=D)
                    tiles = slice(o * OCT, (o + 1) * OCT)
                    link(nc.vector.tensor_tensor(tmp[:, :, :], w,
                                                 pd[:, tiles].unsqueeze(2).to_broadcast([P, OCT, D]), ALU.mult))
                    nc.vector.tensor_tensor(evec[:, tiles, :], tmp[:, :, :], h0[:, tiles, :],
                                            ALU.add).then_inc(e_ready, 1)
                    dve.wait_ge(e_ready, o + 1)
                o = step - 4
                if 0 <= o < NO:
                    tiles = slice(o * OCT, (o + 1) * OCT)
                    dve.wait_ge(e_hi, o + 1)
                    nc.vector.tensor_tensor(e_hl[:, tiles, D:P], evec[:, tiles, :], f32(e_hl[:, tiles, 0:D]),
                                            ALU.subtract).then_inc(e_split, 1)

            def lo_strip(s, k):
                dve.wait_ge(hi_ready, s + 1)
                nc.vector.tensor_tensor(lo[:, k, :], psT[:, k, :], f32(hi[:, k, :]), ALU.subtract).then_inc(lo_ready, 1)

            def t_low(j, b):
                dve.wait_ge(t_hi, j)
                nc.vector.tensor_tensor(tT[:, b, :, D:P], t_rows[:, :, :], f32(tT[:, b, :, 0:D]),
                                        ALU.subtract).then_inc(t_split, 1)

            def add_group(j, g, b):
                dve.wait_ge(acc_free, j * 10 + 2)
                dve.wait_ge(strip_used, j * SA + g * 2 + 2)
                rows = bass.ds(g * RB, RB)
                nc.vector.tensor_tensor(hacc[:, rows], acc[:, b, :], hacc[:, rows], ALU.add).then_inc(acc_free, 1)

            for k in range(4):
                lo_strip(k, k)
            t_low(1, 0)
            dve.wait_ge(acc_free, 2)

            def block_a(j, b, final=False):
                with dve.Fori(0, CA - 1) as c:
                    for k in range(4):
                        lo_strip(j * SA + c * 4 + 4 + k, k)
                        if k % 2:
                            add_group(j, c * 2 + k // 2, k // 2)
                for k in range(4):
                    if k == 3 and not final:
                        t_low(j + 2, 1 - b)
                    if not final:
                        lo_strip(j * SA + SA + k, k)
                    if k % 2:
                        add_group(j, 2 * (CA - 1) + k // 2, k // 2)

            with dve.Fori(0, NJ // 2 - 1) as it:
                block_a(it * 2, 0)
                block_a(it * 2 + 1, 1)
            block_a(NJ - 2, 0)
            block_a(NJ - 1, 1, final=True)

            dve.wait_ge(xr_ready, 1)
            for step in range(NO + 6):
                o = step
                if o < NO:
                    dve.wait_ge(h_row, o + 1)
                    if o >= 2:
                        dve.wait_ge(std2, o - 1)
                    statistics(lambda m: psT[:, o % 4, m * D:(m + 1) * D], 0, o % 2, mean2)
                o = step - 1
                if 0 <= o < NO:
                    dve.wait_ge(std2, o + 1)
                    if o >= 2:
                        dve.wait_ge(hn_ready, o - 1)
                    scales(0, o % 2, rs2)
                o = step - 2
                if 0 <= o < NO:
                    tiles = slice(o * OCT, (o + 1) * OCT)
                    dve.wait_ge(hn_ready, o + 1)
                    link(nc.vector.tensor_tensor(tmp[:, :, :], tmp[:, :, :],
                                                 vecs[:, 0:1, :].to_broadcast([P, OCT, D]), ALU.mult))
                    link(nc.vector.tensor_tensor(outacc[:, tiles, :], tmp[:, :, :], part[:, tiles, :], ALU.add))
                    if o >= 2:
                        dve.wait_ge(std3, o - 1)
                    statistics(lambda m: outacc[:, o * OCT + m, :], 1, o % 2, x1_ready)
                o = step - 3
                if 0 <= o < NO:
                    dve.wait_ge(std3, o + 1)
                    if o >= 2:
                        dve.wait_ge(T0_ready, o - 1)
                    scales(1, o % 2, rs3)
                o = step - 4
                if 0 <= o < NO:
                    tiles = slice(o * OCT, (o + 1) * OCT)
                    dve.wait_ge(T0_hi, o + 1)
                    nc.vector.tensor_tensor(vw_lo[:, tiles, 0:D], T0[:, o % 2, :, :], f32(vw_hi[:, tiles, 0:D]),
                                            ALU.subtract).then_inc(T0_lo, 1)
                    link(nc.vector.tensor_tensor(outacc[:, tiles, :], outacc[:, tiles, :],
                                                 vecs[:, 2:3, :].to_broadcast([P, OCT, D]), ALU.add))
                o = step - 5
                if 0 <= o < NO:
                    tiles = slice(o * OCT, (o + 1) * OCT)
                    dve.wait_ge(T0_w, o + 1)
                    w = fin[:, o % 2 * RB:(o % 2 + 1) * RB].rearrange("p (m d) -> p m d", d=D)
                    nc.vector.tensor_tensor(outacc[:, tiles, :], w, outacc[:, tiles, :], ALU.add).then_inc(T0_out, 1)
            dve.wait_ge(T0_out, NO)

            def event_b(row):
                rows = bass.ds(row * TB, TB)
                dve.wait_ge(fin_a, row + 1)
                nc.vector.tensor_tensor(vw_lo[:, rows, D:P], fin4[:, :, 0:D], f32(vw_hi[:, rows, D:P]),
                                        ALU.subtract).then_inc(rows_ready, 1)
                nc.vector.tensor_tensor(outacc[:, rows, :], fin4[:, :, D:2 * D], outacc[:, rows, :],
                                        ALU.add).then_inc(fin_v, 1)

            def event_c(r):
                rows = bass.ds((NB - 1) * TB - r * TB, TB)
                dve.wait_ge(fin_ready, r + (NB + 1))
                dve.wait_ge(fin_a, NB)
                dve.wait_ge(rows_ready, r + NB)
                nc.vector.tensor_tensor(t2[:, :, :], fin4[:, :, 0:D], part[:, rows, :], ALU.add).then_inc(dchain, 1)
                dve.wait_ge(dchain, r * 2 + (link_at[0] + 1))
                nc.vector.scalar_tensor_tensor(out=t2[:, :, :], in0=t2[:, :, :], scalar=2.0,
                                               in1=f32(vw_hi[:, rows, 0:D]),
                                               op0=ALU.mult, op1=ALU.subtract).then_inc(dchain, 1)
                dve.wait_ge(dchain, r * 2 + (link_at[0] + 2))
                nc.vector.tensor_tensor(t2[:, :, :], t2[:, :, :], f32(vw_lo[:, rows, 0:D]),
                                        ALU.subtract).then_inc(t2_ready, 1)
                nc.vector.tensor_tensor(outacc[:, rows, :], fin4[:, :, D:2 * D], outacc[:, rows, :],
                                        ALU.add).then_inc(fin_v, 1)
                dve.wait_ge(rows_hi, r + (NB + 1))
                nc.vector.tensor_tensor(uw_lo[:, rows, 0:D], t2[:, :, :], f32(uw_hi[:, rows, 0:D]),
                                        ALU.subtract).then_inc(rows_ready, 1)

            def event_d(r, n):
                rows = bass.ds(r * TB, TB)
                dve.wait_ge(fin_ready, n + (2 * NB + 1))
                nc.vector.tensor_tensor(outacc[:, rows, :], fin4[:, :, 0:D], outacc[:, rows, :],
                                        ALU.add).then_inc(out_ready, 1)

            def row_of_strips(base, chunks, event, urgent=False):
                if urgent:
                    event()
                for k in range(4):
                    lo_strip(base + (4 + k), k)
                    if k == 1 and not urgent:
                        event()
                if not isinstance(chunks, int) or chunks > 1:
                    with dve.Fori(1, chunks) as c:
                        for k in range(4):
                            lo_strip(base + c * 4 + (4 + k), k)

            for k in range(4):
                lo_strip(S_B + k, k)
            with dve.Fori(0, NB) as c:
                for k in range(4):
                    lo_strip(c * 4 + (S_B + 4 + k), k)
            with dve.Fori(1, NB) as r:
                row_of_strips(dve.snap(r * (4 * NB) + S_B), NB, lambda: event_b(r - 1))
            row_of_strips(S_C, 1, lambda: event_b(NB - 1), urgent=True)
            dve.wait_ge(fin_v, NB)
            row_of_strips(S_C + 4, 2, lambda: event_c(0), urgent=True)
            with dve.Fori(2, NB) as r:
                row_of_strips(dve.snap(r * (r + 1) * 2 + S_C), r + 1, lambda: event_c(r - 1))
            row_of_strips(S_D, NB, lambda: event_c(NB - 1), urgent=True)
            dve.wait_ge(fin_v, 2 * NB)
            row_of_strips(S_D + 4 * NB, 1, lambda: event_d(NB - 1, 0))
            with dve.Fori(1, PAIRS - 1) as m:
                row_of_strips(dve.snap(m * (4 * (NB + 1)) + S_D), NB - m, lambda: event_d(m - 1, m * 2 - 1))
                row_of_strips(dve.snap(m * (4 * NB) + (S_D + 4 * NB)), m + 1, lambda: event_d(m * -1 + (NB - 1), m * 2))
            row_of_strips(S_END - 4 * (NB + 1), PAIRS + 1, lambda: event_d(PAIRS - 2, NB - 3))
            row_of_strips(S_END - 4 * PAIRS, PAIRS - 1, lambda: event_d(PAIRS, NB - 2))
            event_d(PAIRS - 1, NB - 1)

        @block.tensor
        def _(pe):
            mm = nc.tensor.matmul
            pe.wait_ge(const_ready, 2)
            pe.wait_ge(par_in, 16 * 7)
            nc.tensor.transpose(psT[:, 0, 0:NT], dg_row[:, :], ident[0:NT, 0:NT]).then_inc(pd_t, 1)

            def turn(src, done):
                for m in range(OCT):
                    last = nc.tensor.transpose(acc[0:D, m // 4, m % 4 * P:(m % 4 + 1) * P], src[:, m, :],
                                               ident[:, :])
                last.then_inc(done, 1)

            def times(w, o, done):
                for m in range(OCT):
                    at = o % 2 * RB + m * D
                    last = mm(fin[:, at:at + D], hT[:, m * P:(m + 1) * P], w, start=True, stop=True)
                last.then_inc(done, 1)

            pe.wait_ge(w_in, 64)
            for o in range(NO):
                pe.wait_ge(h0_ready, o + 1)
                if o:
                    pe.wait_ge(h0_tc, o)
                turn(h0[:, o * OCT:(o + 1) * OCT, :], h0_t)
                pe.wait_ge(h0_tc, o + 1)
                if o >= 2:
                    pe.wait_ge(e_ready, o - 1)
                times(w_ui[:, 0 if o * OCT * P < NU else 1, :], o, h0_w)

            def t_product(u, slot, m, leaves=None):
                pe.wait_ge(n_lo_ready, u + 1)
                for i in range(2):
                    rt = slot % CA * 8 + m * 2 + i
                    for a, low in ((n_hi, False), (n_lo, True)):
                        last = mm(fin[:, 0:CW], e_hl[:, rt, :], a[:, m, i * CW:(i + 1) * CW],
                                  start=rt == 0 and not low, stop=rt == NT - 1 and low)
                        if leaves is not None and i == 0 and not low:
                            last.then_inc(leaves, 1)
                        if rt == NT - 1 and not low:
                            last.then_inc(n_used, 1)
                if rt == NT - 1:
                    last.then_inc(t_ready, 1)
                else:
                    last.then_inc(n_used, 1)

            def t_finish(j):
                pe.wait_ge(t_copied, j)
                for i in range(2):
                    last = mm(t_rows[:, i, :], tS[:, i * P:(i + 1) * P], r_sum[:, :], start=True, stop=True)
                last.then_inc(t_row, 1)

            def transpose_a(slot, k):
                for m in range(4):
                    at = ((k // 2) * 4 + m) * CW + (k % 2) * P
                    last = nc.tensor.transpose(psT[:, k, m * P:(m + 1) * P], nat[:, slot, at:at + P], ident[:, :])
                last.then_inc(transposed, 1)

            def block_a(j, b, last_block=False, ahead_two=True):
                slot0, next0 = b * CA, (1 - b) * CA
                for q in range(SA):
                    c, k = q // 4, q % 4
                    if q == 0:
                        pe.wait_ge(t_split, j + 1)
                    pe.wait_ge(lo_ready, j * SA + q + 1)
                    ahead = not (last_block and q >= SA - 4)
                    next_slot = slot0 + c + 1 if c < CA - 1 else next0
                    if ahead:
                        transpose_a(next_slot, k)
                    bank, tile = k // 2, k % 2
                    if tile == 0:
                        pe.wait_ge(acc_free, j * 10 + q // 2 + 1)
                    first = mm(acc[:, bank, :], tT[:, b, tile, :], hi[:, k, :], start=tile == 0, stop=False)
                    if ahead and k == 3:
                        first.then_inc(slot_used[next_slot], 1)
                    mm(acc[:, bank, :], tT[:, b, tile, :], lo[:, k, :], start=False, stop=tile == 1).then_inc(strip_used, 1)
                    if not last_block:
                        if q == Q_NEXT:
                            t_finish(j + 2)
                        for n, u in pieces_beside(q):
                            if n == 1 or ahead_two:
                                t_product((j + n) * UA + u, (next0 if n == 1 else slot0) + u // NR, u % NR)

            pe.wait_ge(e_split, NO)
            pe.wait_ge(consts, 11)
            for u in range(NR):
                t_product(u, 0, u)
            for k in range(4):
                transpose_a(0, k)
            for u in range(NR, UA):
                t_product(u, u // NR, u % NR, slot_used[0] if u == NR else None)
            t_finish(1)
            for u in range(SA - Q_NEXT):
                t_product(UA + u, CA, u)
            with pe.Fori(0, NJ // 2 - 1) as it:
                block_a(it * 2, 0)
                block_a(it * 2 + 1, 1)
            block_a(NJ - 2, 0, ahead_two=False)
            block_a(NJ - 1, 1, last_block=True)

            pe.wait_ge(acc_free, 10 * NJ + 2)
            for step in range(NO + 4):
                o = step
                if o < NO:
                    if o >= 4:
                        pe.wait_ge(hn_ready, o - 3)
                    for m in range(OCT):
                        last = mm(psT[:, o % 4, m * D:(m + 1) * D], hacc[:, (o * OCT + m) * P:(o * OCT + m + 1) * P],
                                  r_sum[:, :], start=True, stop=True)
                    last.then_inc(h_row, 1)
                o = step - 4
                if 0 <= o < NO:
                    pe.wait_ge(T0_ready, o + 1)
                    if o:
                        pe.wait_ge(T0_tc, o)
                    turn(T0[:, o % 2, :, :], T0_t)
                    pe.wait_ge(T0_tc, o + 1)
                    if o >= 2:
                        pe.wait_ge(T0_out, o - 1)
                    times(w_0[:, :], o, T0_w)

            def transpose_b(slot, k, level=None):
                if level is not None:
                    pe.wait_ge(loaded[slot], level)
                for m in range(TB):
                    at = m * RB + k * P
                    last = nc.tensor.transpose(psT[:, k, m * P:(m + 1) * P], nat[:, slot, at:at + P], ident[:, :])
                last.then_inc(transposed, 1)

            def products(phase, j, k, bank, start, stop, leaves=None):
                n = TB * j + k
                if phase == "B":
                    terms = [(vw_hi, hi), (vw_lo, hi), (vw_hi, lo)]
                elif phase == "C":
                    terms = [(uw_hi, hi), (uw_lo, hi), (uw_hi, lo)]
                else:
                    terms = [(vw_hi, hi), (vw_hi, lo)]
                for i, (v, a) in enumerate(terms):
                    last = mm(acc[:, bank, :], v[:, n, :], a[:, k, :], start=start and i == 0,
                              stop=stop and i == len(terms) - 1)
                    if i == 0 and leaves is not None:
                        last.then_inc(leaves, 1)
                last.then_inc(strip_used, 1)

            def finish(row, rhs):
                pe.wait_ge(acc_copied, row + 1)
                for m in range(TB):
                    last = mm(fin4[:, m, 0:rhs.shape[1]], accS[:, m * P:(m + 1) * P], rhs[:, :], start=True, stop=True)
                last.then_inc(fin_ready, 1)

            def chunk(phase, j, bank, strip, ahead, level, first=False, last=False, close=None, urgent=False,
                      prior=None):
                def t(k):
                    if ahead is not None:
                        pe.wait_ge(lo_ready, strip + (k + 1))
                        transpose_b(ahead, k, level if k == 0 else None)

                def p(k):
                    if ahead is None:
                        pe.wait_ge(lo_ready, strip + (k + 1))
                    leaves = None
                    if k == 3 and ahead is not None:
                        leaves = slot_used[ahead]
                    if k == 0 and prior is not None:
                        leaves = slot_used[prior]
                    products(phase, j, k, bank, first and k == 0, last and k == 3, leaves)

                t(0)
                if close is not None and urgent:
                    t(1)
                    close()
                    p(0)
                else:
                    p(0)
                    t(1)
                p(1)
                if close is not None and not urgent:
                    close()
                for k in (2, 3):
                    t(k)
                    p(k)

            def level_b(r):
                return r * 16 + 16 * (NB + 1)

            pe.wait_ge(T0_lo, NO)
            pe.wait_ge(T0_out, NO)
            pe.wait_ge(T0_hi, NO)
            pe.wait_ge(vw_zeroed, 2)
            for k in range(4):
                transpose_b(NB - 1, k, level_b(0) if k == 0 else None)

            def row_b(r, b, base, **head):
                chunk("B", NB - 1, b, base, NB - 2, level_b(r), first=True, **head)
                for j in reversed(range(1, NB - 1)):
                    if j == NB - 3 + b and "close" in head:
                        pe.wait_ge(rows_ready, r)
                        pe.wait_ge(fin_v, r)
                    chunk("B", j, b, base + 4 * (NB - 1 - j), j - 1, level_b(r))
                chunk("B", 0, b, base + 4 * (NB - 1), NB - 1, level_b(r + 1), last=True)

            row_b(0, 0, S_B, prior=NB - 1)
            row_b(1, 1, S_B + 4 * NB, close=lambda: finish(0, r_B))
            with pe.Fori(1, PAIRS) as q:
                for b in (0, 1):
                    row_b(q * 2 + b, b, pe.snap(q * (8 * NB) + (S_B + 4 * NB * b)),
                          close=lambda: finish(q * 2 + (b - 1), r_B))

            def close_last_b():
                finish(NB - 1, r_B)
                pe.wait_ge(uw_ready, 2 * NB)

            def close_c(r):
                pe.wait_ge(fin_v, r + (NB - 1))
                pe.wait_ge(fin_a, NB)
                finish(r + (NB - 1), r_C)

            def close_first_c():
                close_c(1)
                pe.wait_ge(rows_ready, NB + 1)

            strip, slot = S_C, NB - 1
            for r in range(HEAD):
                for j in reversed(range(NB - 1 - r, NB)):
                    slot -= 1
                    ahead, level = (slot, 16 * (2 * NB + 1)) if slot >= 0 else (NB - 1, 16 * (2 * NB + 2))
                    head = {}
                    if j == NB - 1:
                        head = dict(close=[close_last_b, close_first_c, lambda: close_c(2), lambda: close_c(3)][r],
                                    urgent=r < 2)
                    elif j > NB - 1 - r:
                        pe.wait_ge(rows_ready, 2 * NB - j)
                    chunk("C", j, r % 2, strip, ahead, level, first=j == NB - 1, last=j == NB - 1 - r, **head)
                    strip += 4

            def level_c(j, r):
                return r * 16 + 16 * (2 * NB + 2 - HEAD + min(0, j - (NB - 1 - HEAD)))

            with pe.Fori(HEAD // 2, PAIRS) as q:
                for b in (0, 1):
                    r = q * 2 + b
                    base = pe.snap(r * (r + 1) * 2 + S_C)

                    def more(j, **head):
                        if j < NB - 1:
                            pe.wait_ge(rows_ready, 2 * NB - j)
                        chunk("C", j, b, base + 4 * (NB - 1 - j), j - 1, level_c(j - 1, r), first=j == NB - 1, **head)

                    def diagonal(j):
                        chunk("C", j, b, base + 4 * (NB - 1 - j), NB - 1, level_c(NB - 1, r + 1), last=True)

                    more(NB - 1, close=lambda: close_c(r))
                    for j in reversed(range(NB - HEAD - b, NB - 1)):
                        more(j)
                    for n in range(HEAD // 2, PAIRS):
                        j = NB - 1 - 2 * n - b
                        with pe.If(q == n):
                            diagonal(j)
                        pe.end_ifs()
                        if n < PAIRS - 1:
                            with pe.If(q > n):
                                more(j)
                                more(j - 1)
                            pe.end_ifs()

            def level_d(slot, m):
                return m * 16 + 16 * (used_before_d(slot) + 1)

            def close_last_c():
                pe.wait_ge(fin_v, 2 * NB - 1)
                finish(2 * NB - 1, r_C)
                pe.wait_ge(t2_copied, 2 * NB)

            def close_d(n):
                if isinstance(n, int) and n == 0:
                    pe.wait_ge(fin_v, 2 * NB)
                else:
                    pe.wait_ge(out_ready, n)
                finish(n + 2 * NB, r_D)

            def long_row(m, base, **head):
                def more(j, **head):
                    chunk("D", j, 0, base + 4 * j, NB - 2 - j, level_d(NB - 2 - j, m), first=j == 0, **head)

                def diagonal(j):
                    chunk("D", j, 0, base + 4 * j, 0, level_d(0, m + 1), last=True)

                more(0, **head)
                if isinstance(m, int):
                    for j in range(1, NB - 1 - m):
                        more(j)
                    diagonal(NB - 1 - m)
                    return
                for j in range(1, PAIRS + 1):
                    more(j)
                for j in range(PAIRS + 1, NB - 1):
                    with pe.If(m == NB - 1 - j):
                        diagonal(j)
                    pe.end_ifs()
                    if j < NB - 2:
                        with pe.If(m < NB - 1 - j):
                            more(j)
                        pe.end_ifs()

            def short_row(m, base, head):
                def more(j, **head):
                    chunk("D", j, 1, base + 4 * j, j + 1, level_d(j + 1, m) + 16, first=j == 0, **head)

                def diagonal(j, **head):
                    end = isinstance(m, int) and m == PAIRS - 1
                    chunk("D", j, 1, base + 4 * j, None if end else NB - 1, None if end else level_d(NB - 1, m + 1),
                          last=True, **head)

                if isinstance(m, int):
                    if m == 0:
                        diagonal(0, first=True, **head)
                        return
                    more(0, **head)
                    for j in range(1, m):
                        more(j)
                    diagonal(m)
                    return
                more(0, **head)
                for j in range(1, PAIRS - 1):
                    with pe.If(m == j):
                        diagonal(j)
                    pe.end_ifs()
                    if j < PAIRS - 2:
                        with pe.If(m > j):
                            more(j)
                        pe.end_ifs()

            long_row(0, S_D, close=close_last_c, urgent=True)
            short_row(0, S_D + 4 * NB, dict(close=lambda: close_d(0)))
            with pe.Fori(1, PAIRS - 1) as m:
                long_row(m, pe.snap(m * (4 * (NB + 1)) + S_D), close=lambda: close_d(m * 2 - 1))
                short_row(m, pe.snap(m * (4 * NB) + (S_D + 4 * NB)), dict(close=lambda: close_d(m * 2)))
            long_row(PAIRS - 1, S_END - 4 * (NB + 1), close=lambda: close_d(NB - 3))
            short_row(PAIRS - 1, S_END - 4 * PAIRS, dict(close=lambda: close_d(NB - 2)))
            pe.wait_ge(out_ready, NB - 1)
            finish(3 * NB - 1, r_D)


_NAMES = ["x", "adj", "L0_gnn_W_u", "L0_gnn_diag_u", "L0_gnn_par_u", "L0_gnn_W_i", "L0_gnn_diag_i", "L0_gnn_par_i",
          "L0_gnn_ln_gamma", "L0_gnn_ln_beta", "L1_gnn_weight", "L1_gnn_bias"]


def kernel(**inputs):
    import numpy as np
    import concourse.bacc as bacc
    from concourse import mybir as mb
    from concourse.bass_utils import run_bass_kernel_spmd as run

    nc = bacc.Bacc("TRN2", target_bir_lowering=False, num_devices=1)
    arrays, args = {}, []
    for name in _NAMES:
        a = np.ascontiguousarray(inputs[name])
        arrays[f"in_{name}"] = a
        args.append(nc.dram_tensor(f"in_{name}", a.shape, mb.dt.from_np(a.dtype), kind="ExternalInput").ap())
    args.append(nc.dram_tensor("result", (N, D), F32, kind="ExternalOutput").ap())
    build(nc, *args)
    r = run(nc, [arrays], core_ids=[0])
    return r.results[0]["result"]
```

```python
import concourse.bass as bass
from concourse import mybir
from contextlib import ExitStack

F32 = mybir.dt.float32
F32R = mybir.dt.float32r
ALU = mybir.AluOpType
ACT = mybir.ActivationFunctionType

P = 128
N = 5120
D = 64
NT = N // P
NU = 2048
RB = 512
NB = N // RB
TB = RB // P
CW = 256
CR = 1024
CA = N // CR
NJ = N // CW
SA = CA * 4
OCT = 8
NO = NT // OCT
EPS = 1e-5
NR = 4
UA = NT // 2
Q_T = 16
Q_NEXT = 17
DVE_PIECES = [9, 11, 13, 15, 17, 19]
HEAD = 4
LEAD = [(8, 8), (9, 9), (7, 7), (8, 9), (7, 9), (7, 8)]
PAIRS = NB // 2

S_B = NJ * SA
S_C = S_B + NB * NB * 4
S_D = S_C + NB * (NB + 1) // 2 * 4
S_END = S_D + NB * (NB + 1) // 2 * 4


def pieces_beside(q):
    first = SA - Q_NEXT
    if q < Q_T:
        share = UA - first
        return [(1, first + n) for n in range(q * share // Q_T, (q + 1) * share // Q_T)]
    return [(2, q - Q_NEXT)] if q >= Q_NEXT else []


def build(nc, x, adj, W_u, diag_u, par_u, W_i, diag_i, par_i, gamma, beta, weight, bias, out):
    ctx = ExitStack()
    with ctx:
        def sb(name, shape, dt=F32):
            return ctx.enter_context(nc.sbuf_tensor(name, shape, dt))

        def pb(name, shape):
            return ctx.enter_context(nc.psum_tensor(name, shape, F32))

        def sem(name):
            return ctx.enter_context(nc.semaphore(name))

        nat = sb("nat", [P, NB, 2048])
        rowwise = ExitStack()
        hT = rowwise.enter_context(nc.sbuf_tensor("hT", [D, 2, OCT * P], F32))
        tmp = rowwise.enter_context(nc.sbuf_tensor("tmp", [P, OCT, D], F32))
        stats = rowwise.enter_context(nc.sbuf_tensor("stats", [P, 2, 2, OCT, 6], F32))
        w_ui = rowwise.enter_context(nc.sbuf_tensor("w_ui", [D, 2, D], F32))
        dg_row = rowwise.enter_context(nc.sbuf_tensor("dg_row", [NT, P], F32))
        rowwise.close()
        hi = sb("hi", [P, 4, RB], F32R)
        lo = sb("lo", [P, 4, RB], F32R)
        phase_a = ExitStack()
        e_hl = phase_a.enter_context(nc.sbuf_tensor("e_hl", [P, NT, P], F32R))
        n_hi = phase_a.enter_context(nc.sbuf_tensor("n_hi", [P, NR, 2 * CW], F32R))
        n_lo = phase_a.enter_context(nc.sbuf_tensor("n_lo", [P, NR, 2 * CW], F32R))
        tS = phase_a.enter_context(nc.sbuf_tensor("tS", [P, CW], F32))
        phase_a.close()
        vw = sb("vw", [P, NT, 2 * P], F32R)
        vw_hi = vw[:, :, 0:P]
        vw_lo = vw[:, :, P:2 * P]
        T0_hl = vw[:, :, :].rearrange("p t (e v) -> p t v e", v=2)[:, :, 0, :]
        (T0h, T1h), (T0l, T1l) = ([v.rearrange("p t (d v) -> p v t d", v=2)[:, n] for n in range(2)]
                                  for v in (vw_hi, vw_lo))
        outacc = sb("outacc", [P, NT, D])
        part = sb("part", [P, NT, D])
        ident = sb("ident", [P, P])
        r_sum_0 = sb("r_sum_0", [P, 3 * D])
        r_sum = r_sum_0[:, 0:D]
        r_B = sb("r_B", [P, 3 * D])
        r_C = sb("r_C", [P, 2 * D])
        r_D = sb("r_D", [P, D])
        w_01 = sb("w_01", [P, D])
        with nc.sbuf_tensor("wk", [P, 4, D], F32) as wk:
            pass
        t2 = sb("t2", [P, TB, D])
        vecs = sb("vecs", [P, 3, D])
        par = sb("par", [P, 2, 2])
        pd = sb("pd", [P, NT])
        par_p = sb("par_p", [P, 2])
        eps = sb("eps", [P, 1])
        with nc.sbuf_tensor("tT", [P, 2, 2, P], F32R) as tT:
            pass
        with nc.sbuf_tensor("accX", [P, RB], F32) as accX:
            pass
        pairT = sb("pairT", [P, RB])
        accS = sb("accS", [P, RB])
        pair = sb("pair", [P, TB, P])
        mv = sb("mv", [P, 2, 2, OCT, 2])
        rs = sb("rs", [P, 2, 2, OCT])
        nmr = sb("nmr", [P, 2, 2, OCT])
        std = sb("std", [P, 2, 2, OCT])
        early = ExitStack()

        hacc = early.enter_context(nc.sbuf_tensor("hacc", [P, N], F32))
        layer_0 = ExitStack()
        evec = layer_0.enter_context(nc.sbuf_tensor("evec", [P, NT, D], F32))
        h0 = layer_0.enter_context(nc.sbuf_tensor("h0", [P, NT, D], F32))
        layer_0.close()
        tmp2 = early.enter_context(nc.sbuf_tensor("tmp2", [P, 2, OCT, D], F32))
        T0 = early.enter_context(nc.sbuf_tensor("T0", [P, 2, OCT, D], F32))
        stats2 = early.enter_context(nc.sbuf_tensor("stats2", [P, 2, 2, OCT, 6], F32))
        early.close()
        uw_hi = sb("uw_hi", [P, NT, P], F32R)
        uw_lo = sb("uw_lo", [P, NT, P], F32R)
        xin = outacc

        psT = pb("psT", [P, 4, RB])
        acc = pb("acc", [P, 2, RB])
        fin = pb("fin", [P, 2 * RB])

        loaded = [sem(f"loaded{s}") for s in range(NB)]
        slot_used = [sem(f"slot_used{s}") for s in range(NB)]
        x_in = [sem(f"x_in{o}") for o in range(NO)]
        vecs_in, par_in, w_in, w2_in = sem("vecs_in"), sem("par_in"), sem("w_in"), sem("w2_in")
        const_ready, consts = sem("const_ready"), sem("consts")
        pd_t, pd_ready = sem("pd_t"), sem("pd_ready")
        dchain, pchain = sem("dchain"), sem("pchain")
        transposed, hi_ready, lo_ready, strip_used = (
            sem("transposed"), sem("hi_ready"), sem("lo_ready"), sem("strip_used"))
        n_hi_ready, n_lo_ready, n_used = sem("n_hi_ready"), sem("n_lo_ready"), sem("n_used")
        n_lo_dve = sem("n_lo_dve")
        t_ready, t_copied, t_row, t_hi, t_split = (sem(n) for n in ("t_ready", "t_copied", "t_row", "t_hi", "t_split"))
        e_hi, e_split = sem("e_hi"), sem("e_split")
        acc_free = sem("acc_free")
        mean1, std1, rs1, h0_ready, h0_t, h0_tc, h0_w, e_ready = (sem(n) for n in (
            "mean1", "std1", "rs1", "h0_ready", "h0_t", "h0_tc", "h0_w", "e_ready"))
        xr_ready = sem("xr_ready")
        h_row, mean2, std2, rs2, hn_ready, x1_ready, std3, rs3, T0_ready, T0_hi, T0_lo = (
            sem(n) for n in ("h_row", "mean2", "std2", "rs2", "hn_ready", "x1_ready", "std3", "rs3", "T0_ready",
                             "T0_hi", "T0_lo"))
        uw_zeroed, biased = sem("uw_zeroed"), sem("biased")
        x_copied, pair_ready, pair_t, pair_copied = (sem(n) for n in ("x_copied", "pair_ready", "pair_t", "pair_copied"))
        acc_copied, fin_ready, fin_a, fin_v, rows_hi, rows_ready, uw_ready, t2_ready, t2_copied = (sem(n) for n in (
            "acc_copied", "fin_ready", "fin_a", "fin_v", "rows_hi", "rows_ready", "uw_ready", "t2_ready",
            "t2_copied"))
        out_ready, out_sent = sem("out_ready"), sem("out_sent")

        def f32(ap):
            return ap.bitcast(F32)

        fin4 = fin[:, :].rearrange("p (m c) -> p m c", m=TB)
        t_rows = fin[:, RB:RB + 2 * D].rearrange("p (j d) -> p j d", j=2)
        pair_dv = pair[:, :, :].rearrange("p m (v d) -> p m d v", v=2)
        pd_row = fin[:, RB:RB + NT]

        def h_rows(o):
            return (fin[:, 0:RB], fin[:, RB:2 * RB], acc[:, 0, :])[o % 3]

        def turned(o):
            return (acc if o % 2 == 0 else psT)[0:D, 0:2, :]

        out_v = out.rearrange("(t p) d -> p t d", p=P)
        x_v = x.rearrange("(t p) d -> p t d", p=P)

        def used_before_d(slot):
            return 2 * NB + 1 + min(NB - HEAD, slot + 1)

        head_c = LEAD + [(NB - HEAD, j) for j in reversed(range(NB - HEAD, NB))]

        block = ctx.enter_context(nc.Block())

        @block.sync
        def _(sp):
            for o in range(NO):
                tiles = slice(o * OCT, (o + 1) * OCT)
                sp.dma_start(xin[:, tiles, :], x_v[:, tiles, :]).then_inc(x_in[o], 16)
            sp.dma_start(w_ui[:, 0, :], W_u).then_inc(w_in, 16)
            sp.dma_start(w_ui[:, 1, :], W_i).then_inc(w_in, 16)
            sp.dma_start(wk[0:D, :, :], weight.rearrange("k i o -> i k o")).then_inc(w_in, 16)
            sp.dma_start(wk[D:P, :, :], weight.rearrange("k i o -> i k o")).then_inc(w_in, 16)
            adj_a = adj.rearrange("(c m p) n -> c p m n", p=P, m=CR // P)
            adj_b = adj.rearrange("(i m p) n -> i p m n", p=P, m=TB)

            def slot_left(slot, uses):
                if not isinstance(uses, int):
                    sp.lower_val(uses)
                sp.wait_ge(w_in, 64)
                sp.wait_ge(slot_used[slot], uses)

            def load_a(slot, c, col, uses=None):
                dst = nat[:, slot, :].rearrange("p (m n) -> p m n", n=CW)
                src = adj_a[c, :, :, bass.ds(col, CW)]
                if uses is not None:
                    slot_left(slot, uses)
                sp.dma_start(dst, src).then_inc(loaded[slot], 16)

            def load_b(j, row, uses, slot=None):
                slot = j if slot is None else slot
                dst = nat[:, slot, :].rearrange("p (m n) -> p m n", n=RB)
                src = adj[bass.ds(row, RB), j * RB:(j + 1) * RB].rearrange("(m p) n -> p m n", p=P)
                slot_left(slot, uses)
                sp.dma_start(dst, src).then_inc(loaded[slot], 16)

            for slot in range(NB):
                load_a(slot, slot % CA, slot // CA * CW)
            for n, v in enumerate((gamma, beta, bias)):
                sp.dma_start(vecs[:, n, :], v.rearrange("(a n) -> a n", a=1).to_broadcast([P, D])).then_inc(vecs_in, 16)
            with sp.Fori(1, NJ // 2) as it:
                for slot in range(NB):
                    load_a(slot, slot % CA, it * (2 * CW) + slot // CA * CW, it)
            with sp.Fori(0, NB) as r:
                for j in reversed(range(NB)):
                    load_b(j, r * RB, r + NB)
            for n, (row, j) in enumerate(head_c):
                load_b(j, row * RB, 2 * NB, NB - 1 - n)
            with sp.Fori(HEAD, NB) as r:
                row = (NB - 1) * RB - r * RB
                for j in reversed(range(NB)):
                    if j >= NB - 1 - HEAD:
                        load_b(j, row, r + (2 * NB + 1 - HEAD))
                    else:
                        with sp.If(r > NB - 2 - j):
                            load_b(j, row, r + (NB + 2 + j))
                        sp.end_ifs()
            with sp.Fori(0, PAIRS) as m:
                for j in reversed(range(NB)):
                    if j <= PAIRS:
                        load_b(j, (NB - 1) * RB - m * RB, m + used_before_d(j))
                    else:
                        with sp.If(m < NB - j):
                            load_b(j, (NB - 1) * RB - m * RB, m + used_before_d(j))
                        sp.end_ifs()
                for j in range(PAIRS):
                    slot = NB - 1 - j
                    if j == 0:
                        load_b(j, m * RB, m + (used_before_d(slot) + 1), slot)
                    else:
                        with sp.If(m > j - 1):
                            load_b(j, m * RB, m + (used_before_d(slot) + 1), slot)
                        sp.end_ifs()

        @block.gpsimd
        def _(pool):
            nc.gpsimd.memset(r_B[:, :], 0.0).then_inc(pchain, 1)
            nc.gpsimd.memset(ident[:, :], 0.0).then_inc(pchain, 1)
            nc.gpsimd.memset(eps[:, :], EPS).then_inc(const_ready, 1)
            pool.wait_ge(pchain, 2)
            nc.gpsimd.affine_select(out=ident[:, :], in_=ident[:, :], compare_op=ALU.not_equal, fill=1.0, base=0,
                                    pattern=[[-1, P]], channel_multiplier=1).then_inc(const_ready, 1)
            nc.gpsimd.memset(hacc[:, 0:N // 2], 0.0).then_inc(acc_free, 1)
            nc.gpsimd.memset(hacc[:, N // 2:N], 0.0).then_inc(acc_free, 1)
            nc.gpsimd.memset(r_C[:, :], 0.0).then_inc(pchain, 1)
            nc.gpsimd.memset(r_sum_0[:, :], 0.0).then_inc(pchain, 1)
            pool.wait_ge(const_ready, 2)
            pool.wait_ge(pchain, 4)
            pool.wait_ge(w_in, 64)
            for h in (slice(0, D), slice(D, P)):
                nc.gpsimd.tensor_copy(r_sum_0[h, 0:D], ident[h, h]).then_inc(consts, 1)
            pool.wait_ge(consts, 2)
            halves = ident[:, :].rearrange("p (d v) -> p v d", v=2)
            nc.gpsimd.tensor_copy(r_B[:, 0:D], halves[:, 0, :]).then_inc(consts, 1)
            pool.wait_ge(consts, 3)
            nc.gpsimd.tensor_copy(r_B[:, 2 * D:3 * D], halves[:, 1, :]).then_inc(consts, 1)
            pool.wait_ge(consts, 4)
            nc.gpsimd.tensor_copy(r_C[D:P, 0:D], ident[D:P, D:P]).then_inc(consts, 1)
            nc.gpsimd.tensor_tensor(w_01[D:P, :], wk[D:P, 1, :], wk[D:P, 3, :], ALU.subtract).then_inc(consts, 1)
            nc.gpsimd.tensor_tensor(w_01[0:D, :], wk[0:D, 0, :], wk[0:D, 2, :], ALU.subtract).then_inc(consts, 1)
            pool.wait_ge(w2_in, 16)
            pool.wait_ge(consts, 7)
            nc.gpsimd.tensor_tensor(r_B[:, D:2 * D], r_B[:, D:2 * D], r_B[:, D:2 * D], ALU.add).then_inc(consts, 1)
            pool.wait_ge(consts, 8)
            nc.gpsimd.tensor_tensor(r_C[D:P, D:2 * D], wk[D:P, 2, :], wk[D:P, 2, :], ALU.add).then_inc(consts, 1)
            nc.gpsimd.tensor_tensor(r_C[0:D, D:2 * D], wk[0:D, 3, :], wk[0:D, 3, :], ALU.add).then_inc(consts, 1)
            pool.wait_ge(consts, 10)
            nc.gpsimd.tensor_tensor(r_D[:, :], wk[:, 3, :], wk[:, 3, :], ALU.add).then_inc(consts, 1)
            def n_low(u, slot, m):
                pool.wait_ge(n_hi_ready, u + 1)
                nc.gpsimd.tensor_tensor(n_lo[:, m, :].unsqueeze(1), nat[:, slot, m * 2 * CW:(m + 1) * 2 * CW],
                                        f32(n_hi[:, m, :]).unsqueeze(1), ALU.subtract).then_inc(n_lo_ready, 1)

            for c in range(CA):
                for m in range(NR):
                    if (c * NR + m) not in DVE_PIECES:
                        n_low(c * NR + m, slice(c, c + 1), m)
            with pool.Fori(0, NJ // 2 - 1) as it:
                for b in (1, 0):
                    with pool.Fori(0, CA) as c:
                        for m in range(NR):
                            n_low(it * (2 * UA) + c * NR + ((2 - b) * UA + m), bass.ds(c + b * CA, 1), m)
            with pool.Fori(0, CA) as c:
                for m in range(NR):
                    n_low(c * NR + ((NJ - 1) * UA + m), bass.ds(c + CA, 1), m)
            pool.wait_ge(vecs_in, 16 * 3)
            pool.wait_ge(h0_ready, NO)
            for o in range(NO):
                pool.wait_ge(x_in[o], 16)
            nc.gpsimd.tensor_tensor(part[:, :, :], xin[:, :, :], h0[:, :, :], ALU.add).then_inc(pchain, 1)
            pool.wait_ge(pchain, 5)
            nc.gpsimd.tensor_tensor(part[:, :, :], part[:, :, :],
                                    vecs[:, 1:2, :].to_broadcast([P, NT, D]), ALU.add).then_inc(xr_ready, 1)
            pool.wait_ge(T0_ready, NO)
            nc.gpsimd.tensor_tensor(outacc[:, :, :], outacc[:, :, :],
                                    vecs[:, 2:3, :].to_broadcast([P, NT, D]), ALU.add).then_inc(biased, 1)
            pool.wait_ge(h_row, NO)
            pool.wait_ge(T0_hi, NO)
            pool.wait_ge(T0_lo, NO)
            nc.gpsimd.memset(f32(uw_hi[:, :, 0:D]), 0.0).then_inc(uw_zeroed, 1)
            nc.gpsimd.memset(f32(uw_lo[:, :, 0:D]), 0.0).then_inc(uw_zeroed, 1)
            with pool.Fori(0, NB) as r:
                pool.wait_ge(rows_ready, r + 1)
                rows = bass.ds(r * TB, TB)
                nc.gpsimd.tensor_copy(uw_hi[:, rows, D:P], f32(T1h[:, rows, :])).then_inc(uw_ready, 1)
                nc.gpsimd.tensor_copy(uw_lo[:, rows, D:P], f32(T1l[:, rows, :])).then_inc(uw_ready, 1)
            with pool.Fori(0, NB) as r:
                rows = bass.ds((NB - 1) * TB - r * TB, TB)
                nc.gpsimd.tensor_tensor(pair_dv, f32(vw_hi[:, rows, :]), f32(vw_lo[:, rows, :]),
                                        ALU.add).then_inc(pair_ready, 1)
                pool.wait_ge(pair_ready, r + 1)
                pool.wait_ge(pair_t, r + 1)
                pool.wait_ge(rows_ready, r + NB + 1)
                nc.gpsimd.tensor_copy(vw_hi[:, rows, 0:D], f32(uw_hi[:, rows, 0:D])).then_inc(t2_copied, 1)
                nc.gpsimd.tensor_copy(vw_hi[:, rows, D:P], f32(uw_lo[:, rows, 0:D])).then_inc(t2_copied, 1)
            with pool.Fori(0, PAIRS) as m:
                for b, row in ((0, m * -1 + (NB - 1)), (1, m)):
                    pool.wait_ge(out_ready, m * 2 + (b + 1))
                    pool.dma_start(out[bass.ds(row * RB, RB), :].rearrange("(m p) d -> p m d", p=P),
                                   outacc[:, bass.ds(row * TB, TB), :]).then_inc(out_sent, 16)
            pool.wait_ge(out_sent, 16 * NB)

        @block.scalar
        def _(act):
            act.dma_start(dg_row[0:NU // P, :], diag_u.rearrange("(t p) -> t p", p=P)).then_inc(par_in, 16)
            act.dma_start(dg_row[NU // P:NT, :], diag_i.rearrange("(t p) -> t p", p=P)).then_inc(par_in, 16)
            for n, v in enumerate((par_u, par_i)):
                act.dma_start(par[:, n, :], v.rearrange("(a n) -> a n", a=1).to_broadcast([P, 2])).then_inc(par_in, 16)
            act.wait_ge(pchain, 1)
            act.dma_start(r_B[1:P:2, D:2 * D], weight[2, :, :]).then_inc(w2_in, 16)

            def hi_strip(s, k):
                act.wait_ge(transposed, s + 1)
                act.wait_ge(strip_used, s - 3)
                nc.scalar.activation(hi[:, k, :], psT[:, k, :], ACT.Copy).then_inc(hi_ready, 1)

            def n_high(u, slot, m, level=None, wait=True):
                if level is not None:
                    act.wait_ge(loaded[slot], level)
                if wait:
                    act.wait_ge(n_used, u - (NR - 1))
                nc.scalar.activation(n_hi[:, m, :], nat[:, slot, m * 2 * CW:(m + 1) * 2 * CW],
                                     ACT.Copy).then_inc(n_hi_ready, 1)

            def t_copy(j):
                act.wait_ge(t_ready, j)
                nc.scalar.activation(tS[:, :], fin[:, 0:CW], ACT.Copy).then_inc(t_copied, 1)

            def t_high(j, b):
                act.wait_ge(t_row, j)
                nc.scalar.activation(tT[:, b, :, 0:D], t_rows[:, :, :], ACT.Copy).then_inc(t_hi, 1)

            act.wait_ge(const_ready, 2)
            for step in range(NO + 4):
                o = step - 4
                if 0 <= o < NO:
                    tiles = slice(o * OCT, (o + 1) * OCT)
                    act.wait_ge(e_ready, o + 1)
                    nc.scalar.activation(e_hl[:, tiles, 0:D], evec[:, tiles, :], ACT.Copy).then_inc(e_hi, 1)
                o = step - 1
                if 0 <= o < NO:
                    act.wait_ge(rs1, o + 1)
                    for m in range(OCT):
                        last = nc.scalar.activation(h0[:, o * OCT + m, :], xin[:, o * OCT + m, :], ACT.Relu,
                                                    bias=nmr[:, 0, o % 2, m:m + 1], scale=rs[:, 0, o % 2, m:m + 1])
                    last.then_inc(h0_ready, 1)
                if step < NO:
                    o, b = step, step % 2
                    act.wait_ge(mean1, o + 1)
                    nc.scalar.activation(std[:, 0, b, :], mv[:, 0, b, :, 1], ACT.Sqrt, bias=eps[:, :]).then_inc(std1, 1)
                c = 0 if step == 2 else step - 4 if step > 4 else CA
                if c < CA:
                    for m in range(NR):
                        n_high(c * NR + m, c, m, 16 if m == 0 else None, wait=c > 0)

            for u in range(SA - Q_NEXT):
                n_high(UA + u, CA, u, 16 if u == 0 else None)
            t_copy(1)
            for k in range(4):
                act.wait_ge(transposed, k + 1)
                nc.scalar.activation(hi[:, k, :], psT[:, k, :], ACT.Copy).then_inc(hi_ready, 1)
            t_high(1, 0)
            for q in (0, 1):
                for _, u in pieces_beside(q):
                    n_high(UA + u, CA + u // NR, u % NR, 16 if u % NR == 0 else None)

            def block_a(j, b, level, after, ahead=True, final=False):
                for q in range(16 if final else SA):
                    if q == Q_T and not final:
                        t_copy(j + 2)
                    if q == Q_NEXT + 1 and not final:
                        t_high(j + 2, 1 - b)
                    wraps = q + 2 >= SA
                    for n, u in () if final else pieces_beside((q + 2) % SA):
                        n += wraps
                        slot0, arrived = ((1 - b) * CA, level) if n == 1 else (b * CA, after)
                        if n == 1 or ahead:
                            n_high((j + n) * UA + u, slot0 + u // NR, u % NR, arrived if u % NR == 0 else None)
                    hi_strip(j * SA + (q + 4), q % 4)

            with act.Fori(0, NJ // 2 - 1) as it:
                block_a(it * 2, 0, it * 16 + 16, it * 16 + 32)
                block_a(it * 2 + 1, 1, it * 16 + 32, it * 16 + 32)
            block_a(NJ - 2, 0, NJ // 2 * 16, None, ahead=False)
            block_a(NJ - 1, 1, None, None, final=True)

            def row_0_chunk(o, half):
                for k in range(4):
                    hi_strip(S_B + 4 + o * 8 + half * 4 + k, k)

            for k in range(4):
                hi_strip(S_B + k, k)
            for step in range(NO + 4):
                o = step - 3
                if 0 <= o < NO:
                    tile = (NO - 1 - o) * OCT
                    act.wait_ge(rs3, o + 1)
                    if o >= 2:
                        act.wait_ge(T0_lo, o - 1)
                    for m in range(OCT):
                        last = nc.scalar.activation(T0[:, o % 2, m, :], outacc[:, tile + m, :], ACT.Relu,
                                                    bias=nmr[:, 1, o % 2, m:m + 1], scale=rs[:, 1, o % 2, m:m + 1])
                    last.then_inc(T0_ready, 1)
                    act.wait_ge(T0_ready, o + 1)
                    nc.scalar.activation(T0h[:, tile:tile + OCT, :], T0[:, o % 2, :, :],
                                         ACT.Copy).then_inc(T0_hi, 1)
                o = step
                if o < NO:
                    act.wait_ge(mean2, o + 1)
                    nc.scalar.activation(std[:, 0, o % 2, :], mv[:, 0, o % 2, :, 1], ACT.Sqrt,
                                         bias=eps[:, :]).then_inc(std2, 1)
                if step >= 4:
                    row_0_chunk(step - 4, 0)
                o = step - 1
                if 0 <= o < NO:
                    act.wait_ge(rs2, o + 1)
                    if o >= 2:
                        act.wait_ge(x1_ready, o - 1)
                    for m in range(OCT):
                        last = nc.scalar.activation(tmp2[:, o % 2, m, :], h_rows(o)[:, m * D:(m + 1) * D], ACT.Identity,
                                                    bias=nmr[:, 0, o % 2, m:m + 1], scale=rs[:, 0, o % 2, m:m + 1])
                    last.then_inc(hn_ready, 1)
                o = step - 2
                if 0 <= o < NO:
                    act.wait_ge(x1_ready, o + 1)
                    nc.scalar.activation(std[:, 1, o % 2, :], mv[:, 1, o % 2, :, 1], ACT.Sqrt,
                                         bias=eps[:, :]).then_inc(std3, 1)
                if step >= 4:
                    row_0_chunk(step - 4, 1)

            def copy_acc(strips, bank, row):
                act.wait_ge(strip_used, strips)
                if row is not None:
                    act.wait_ge(fin_ready, row)
                nc.scalar.activation(accS[:, :], acc[:, bank, :], ACT.Copy).then_inc(acc_copied, 1)

            def event_b(row):
                rows = bass.ds(row * TB, TB)
                act.wait_ge(fin_ready, row + 1)
                nc.scalar.activation(T1h[:, rows, :], fin4[:, :, 0:D], ACT.Copy).then_inc(rows_hi, 1)
                nc.scalar.activation(part[:, rows, :], fin4[:, :, 2 * D:3 * D], ACT.Copy).then_inc(fin_a, 1)

            def copy_x(row, strips):
                act.wait_ge(strip_used, strips)
                if row is not None:
                    act.wait_ge(fin_ready, row)
                nc.scalar.activation(accX[:, :], acc[:, 0, :], ACT.Copy).then_inc(x_copied, 1)

            def copy_pair(r):
                act.wait_ge(pair_t, r + 1)
                nc.scalar.activation(pairT[:, :], fin[:, 0:RB], ACT.Copy).then_inc(pair_copied, 1)

            def event_c(r):
                rows = bass.ds((NB - 1) * TB - r * TB, TB)
                act.wait_ge(t2_ready, r + 1)
                nc.scalar.activation(uw_hi[:, rows, 0:D], t2[:, :, :], ACT.Copy).then_inc(rows_hi, 1)

            def row_of_strips(base, chunks, bank, done, event=None, urgent=False, row=None, pair_of=None):
                copy_acc(base, bank, done)
                if urgent:
                    copy_pair(pair_of)
                    event()
                for k in range(4):
                    hi_strip(base + (4 + k), k)
                    if k == 0 and pair_of is not None and not urgent:
                        copy_pair(pair_of)
                    if k == 1 and event is not None and not urgent:
                        event()
                if not isinstance(chunks, int) or chunks > 1:
                    with act.Fori(1, chunks) as c:
                        if row is not None:
                            with act.If(c == NB - row):
                                copy_x(row, base + c * 4)
                            act.end_ifs()
                        for k in range(4):
                            hi_strip(base + c * 4 + (4 + k), k)

            row_of_strips(S_B + 4 * NB, NB, 1, None, lambda: event_b(0), row=1)
            with act.Fori(2, NB) as r:
                row_of_strips(act.snap(r * (4 * NB) + S_B), NB, 1, r - 1, lambda: event_b(r - 1), row=r)
            row_of_strips(S_C, 2, 1, NB - 1, lambda: event_b(NB - 1))
            act.wait_ge(uw_zeroed, 2)
            row_of_strips(S_C + 8, 2, 1, NB, lambda: event_c(0), urgent=True, pair_of=0)
            row_of_strips(S_C + 16, 2, 0, NB + 1, lambda: event_c(1), pair_of=1)
            row_of_strips(S_C + 24, 4, 1, NB + 2, lambda: event_c(2), pair_of=2)
            with act.Fori(HEAD // 2, PAIRS) as q:
                for b in (0, 1):
                    r = q * 2 + b
                    base = act.snap(r * (r + 1) * 2 + S_C)
                    row_of_strips(base, r + 1, b, r + (NB - 1), lambda: event_c(r - 1), pair_of=r - 1)
            row_of_strips(S_D, NB, 0, 2 * NB - 1, lambda: event_c(NB - 1), pair_of=NB - 1)
            row_of_strips(S_D + 4 * NB, 1, 1, 2 * NB)
            with act.Fori(1, PAIRS - 1) as m:
                base = act.snap(m * (4 * (NB + 1)) + S_D)
                row_of_strips(base, NB - m, 0, m * 2 + (2 * NB - 1))
                base = act.snap(m * (4 * NB) + (S_D + 4 * NB))
                row_of_strips(base, m + 1, 1, m * 2 + 2 * NB)
            end = S_END - 4 * (NB + 1)
            row_of_strips(end, PAIRS + 1, 0, 3 * NB - 3)
            row_of_strips(S_END - 4 * PAIRS, PAIRS - 1, 1, 3 * NB - 2)
            copy_acc(S_END, 0, 3 * NB - 1)

        @block.vector
        def _(dve):
            link_at = [0]

            def link(ins):
                link_at[0] += 1
                ins.then_inc(dchain, 1)
                dve.wait_ge(dchain, link_at[0])

            def statistics(src, which, b, done, stats=stats):
                for m in range(OCT):
                    last = nc.vector.bn_stats(stats[:, which, b, m, :], src(m))
                link(last)
                for m in range(OCT):
                    last = nc.vector.bn_aggr(mv[:, which, b, m, :], stats[:, which, b, m, :])
                last.then_inc(done, 1)

            def scales(which, b, done):
                link(nc.vector.reciprocal(rs[:, which, b, :], std[:, which, b, :]))
                nc.vector.scalar_tensor_tensor(out=nmr[:, which, b, :], in0=mv[:, which, b, :, 0], scalar=-1.0,
                                               in1=rs[:, which, b, :], op0=ALU.mult, op1=ALU.mult).then_inc(done, 1)

            def n_low(u, slot, m):
                dve.wait_ge(n_hi_ready, u + 1)
                nc.vector.tensor_tensor(n_lo[:, m, :].unsqueeze(1), nat[:, slot:slot + 1, m * 2 * CW:(m + 1) * 2 * CW],
                                        f32(n_hi[:, m, :]).unsqueeze(1), ALU.subtract).then_inc(n_lo_dve, 1)

            for step in range(NO + 4):
                o = step - 4
                if 0 <= o < NO:
                    tiles = slice(o * OCT, (o + 1) * OCT)
                    dve.wait_ge(e_hi, o + 1)
                    nc.vector.tensor_tensor(e_hl[:, tiles, D:P], evec[:, tiles, :], f32(e_hl[:, tiles, 0:D]),
                                            ALU.subtract).then_inc(e_split, 1)
                o = step - 1
                if 0 <= o < NO:
                    dve.wait_ge(std1, o + 1)
                    if o >= 2:
                        dve.wait_ge(h0_ready, o - 1)
                    scales(0, o % 2, rs1)
                if step == 2:
                    dve.wait_ge(par_in, 16 * 4)
                    link(nc.vector.tensor_tensor(par_p[:, :], par[:, :, 0], par[:, :, 1], ALU.mult))
                    dve.wait_ge(pd_t, 1)
                    nu = NU // P
                    for n, tiles in enumerate((slice(0, nu), slice(nu, NT))):
                        nc.vector.tensor_scalar(pd[:, tiles], pd_row[:, tiles], par_p[:, n:n + 1], None,
                                                ALU.mult).then_inc(pd_ready, 1)
                    dve.wait_ge(pd_ready, 2)
                o = step - 2
                if 0 <= o < NO:
                    dve.wait_ge(h0_t, o + 1)
                    if o >= 2:
                        dve.wait_ge(h0_w, o - 1)
                    nc.vector.tensor_copy(hT[:, o % 2, :], turned(o).rearrange("p a b -> p (a b)")).then_inc(h0_tc, 1)
                o = step - 3
                if 0 <= o < NO:
                    dve.wait_ge(h0_w, o + 1)
                    w = psT[:, 2 + o % 2, :].rearrange("p (m d) -> p m d", d=D)
                    tiles = slice(o * OCT, (o + 1) * OCT)
                    link(nc.vector.tensor_tensor(tmp[:, :, :], w,
                                                 pd[:, tiles].unsqueeze(2).to_broadcast([P, OCT, D]), ALU.mult))
                    nc.vector.tensor_tensor(evec[:, tiles, :], tmp[:, :, :], h0[:, tiles, :],
                                            ALU.add).then_inc(e_ready, 1)
                    dve.wait_ge(e_ready, o + 1)
                o = step
                if o < NO:
                    dve.wait_ge(x_in[o], 16)
                    if o >= 2:
                        dve.wait_ge(std1, o - 1)
                    statistics(lambda m: xin[:, o * OCT + m, :], 0, o % 2, mean1)
                c = step - 4
                if 2 <= c < CA:
                    for m in range(1, NR, 2):
                        n_low(c * NR + m, c, m)

            def lo_strip(s, k):
                dve.wait_ge(hi_ready, s + 1)
                nc.vector.tensor_tensor(lo[:, k, :], psT[:, k, :], f32(hi[:, k, :]), ALU.subtract).then_inc(lo_ready, 1)

            def t_low(j, b):
                dve.wait_ge(t_hi, j)
                nc.vector.tensor_tensor(tT[:, b, :, D:P], t_rows[:, :, :], f32(tT[:, b, :, 0:D]),
                                        ALU.subtract).then_inc(t_split, 1)

            def add_group(j, g, b):
                dve.wait_ge(acc_free, j * 10 + 2)
                dve.wait_ge(strip_used, j * SA + g * 2 + 2)
                rows = bass.ds(g * RB, RB)
                nc.vector.tensor_tensor(hacc[:, rows], acc[:, b, :], hacc[:, rows], ALU.add).then_inc(acc_free, 1)

            for k in range(4):
                lo_strip(k, k)
            t_low(1, 0)
            dve.wait_ge(acc_free, 2)

            def block_a(j, b, final=False):
                with dve.Fori(0, CA - 1) as c:
                    for k in range(4):
                        lo_strip(j * SA + c * 4 + 4 + k, k)
                        if k % 2:
                            add_group(j, c * 2 + k // 2, k // 2)
                for k in range(4):
                    if k == 3 and not final:
                        t_low(j + 2, 1 - b)
                    if not final:
                        lo_strip(j * SA + SA + k, k)
                    if k % 2:
                        add_group(j, 2 * (CA - 1) + k // 2, k // 2)

            with dve.Fori(0, NJ // 2 - 1) as it:
                block_a(it * 2, 0)
                block_a(it * 2 + 1, 1)
            block_a(NJ - 2, 0)
            block_a(NJ - 1, 1, final=True)

            for k in range(4):
                lo_strip(S_B + k, k)
            dve.wait_ge(xr_ready, 1)
            def row_0_chunk(o, half):
                for k in range(4):
                    lo_strip(S_B + 4 + o * 8 + half * 4 + k, k)

            for step in range(NO + 4):
                o = step
                if o < NO:
                    dve.wait_ge(h_row, o + 1)
                    if o >= 2:
                        dve.wait_ge(std2, o - 1)
                    statistics(lambda m: h_rows(o)[:, m * D:(m + 1) * D], 0, o % 2, mean2, stats2)
                if step >= 4:
                    row_0_chunk(step - 4, 0)
                o = step - 1
                if 0 <= o < NO:
                    dve.wait_ge(std2, o + 1)
                    if o >= 2:
                        dve.wait_ge(hn_ready, o - 1)
                    scales(0, o % 2, rs2)
                o = step - 2
                if 0 <= o < NO:
                    tile = (NO - 1 - o) * OCT
                    tiles = slice(tile, tile + OCT)
                    dve.wait_ge(hn_ready, o + 1)
                    link(nc.vector.tensor_tensor(tmp2[:, o % 2, :, :], tmp2[:, o % 2, :, :],
                                                 vecs[:, 0:1, :].to_broadcast([P, OCT, D]), ALU.mult))
                    link(nc.vector.tensor_tensor(outacc[:, tiles, :], tmp2[:, o % 2, :, :], part[:, tiles, :],
                                                 ALU.add))
                    if o >= 2:
                        dve.wait_ge(std3, o - 1)
                    statistics(lambda m: outacc[:, tile + m, :], 1, o % 2, x1_ready, stats2)
                o = step - 3
                if 0 <= o < NO:
                    tiles = slice((NO - 1 - o) * OCT, (NO - o) * OCT)
                    dve.wait_ge(T0_hi, o + 1)
                    nc.vector.tensor_tensor(T0l[:, tiles, :], T0[:, o % 2, :, :], f32(T0h[:, tiles, :]),
                                            ALU.subtract).then_inc(T0_lo, 1)
                o = step - 2
                if 0 <= o < NO:
                    dve.wait_ge(std3, o + 1)
                    if o >= 2:
                        dve.wait_ge(T0_ready, o - 1)
                    scales(1, o % 2, rs3)
                if step >= 4:
                    row_0_chunk(step - 4, 1)
            dve.wait_ge(biased, 1)

            def event_b(row):
                rows = bass.ds(row * TB, TB)
                dve.wait_ge(fin_a, row + 1)
                nc.vector.tensor_tensor(T1l[:, rows, :], fin4[:, :, 0:D], f32(T1h[:, rows, :]),
                                        ALU.subtract).then_inc(rows_ready, 1)
                nc.vector.tensor_tensor(outacc[:, rows, :], fin4[:, :, D:2 * D], outacc[:, rows, :],
                                        ALU.add).then_inc(fin_v, 1)

            def event_c(r):
                rows = bass.ds((NB - 1) * TB - r * TB, TB)
                dve.wait_ge(fin_ready, r + (NB + 1))
                dve.wait_ge(fin_a, NB)
                dve.wait_ge(rows_ready, r + NB)
                nc.vector.tensor_tensor(t2[:, :, :], fin4[:, :, 0:D], part[:, rows, :], ALU.add).then_inc(dchain, 1)
                dve.wait_ge(dchain, r * 2 + (link_at[0] + 1))
                nc.vector.scalar_tensor_tensor(out=t2[:, :, :], in0=t2[:, :, :], scalar=2.0,
                                               in1=f32(T0h[:, rows, :]),
                                               op0=ALU.mult, op1=ALU.subtract).then_inc(dchain, 1)
                dve.wait_ge(dchain, r * 2 + (link_at[0] + 2))
                nc.vector.tensor_tensor(t2[:, :, :], t2[:, :, :], f32(T0l[:, rows, :]),
                                        ALU.subtract).then_inc(t2_ready, 1)
                nc.vector.tensor_tensor(outacc[:, rows, :], fin4[:, :, D:2 * D], outacc[:, rows, :],
                                        ALU.add).then_inc(fin_v, 1)
                dve.wait_ge(rows_hi, r + (NB + 1))
                nc.vector.tensor_tensor(uw_lo[:, rows, 0:D], t2[:, :, :], f32(uw_hi[:, rows, 0:D]),
                                        ALU.subtract).then_inc(rows_ready, 1)

            def event_d(r, n):
                rows = bass.ds(r * TB, TB)
                dve.wait_ge(fin_ready, n + (2 * NB + 1))
                nc.vector.tensor_tensor(outacc[:, rows, :], fin4[:, :, 0:D], outacc[:, rows, :],
                                        ALU.add).then_inc(out_ready, 1)

            def row_of_strips(base, chunks, event, urgent=False):
                if urgent:
                    event()
                for k in range(4):
                    lo_strip(base + (4 + k), k)
                    if k == 1 and not urgent:
                        event()
                if not isinstance(chunks, int) or chunks > 1:
                    with dve.Fori(1, chunks) as c:
                        for k in range(4):
                            lo_strip(base + c * 4 + (4 + k), k)

            with dve.Fori(1, NB) as r:
                row_of_strips(dve.snap(r * (4 * NB) + S_B), NB, lambda: event_b(r - 1))
            row_of_strips(S_C, 2, lambda: event_b(NB - 1))
            dve.wait_ge(fin_v, NB)
            row_of_strips(S_C + 8, 2, lambda: event_c(0), urgent=True)
            row_of_strips(S_C + 16, 2, lambda: event_c(1))
            with dve.Fori(HEAD - 1, NB) as r:
                row_of_strips(dve.snap(r * (r + 1) * 2 + S_C), r + 1, lambda: event_c(r - 1))
            row_of_strips(S_D, NB, lambda: event_c(NB - 1))
            dve.wait_ge(fin_v, 2 * NB)
            row_of_strips(S_D + 4 * NB, 1, lambda: event_d(NB - 1, 0))
            with dve.Fori(1, PAIRS - 1) as m:
                row_of_strips(dve.snap(m * (4 * (NB + 1)) + S_D), NB - m, lambda: event_d(m - 1, m * 2 - 1))
                row_of_strips(dve.snap(m * (4 * NB) + (S_D + 4 * NB)), m + 1, lambda: event_d(m * -1 + (NB - 1), m * 2))
            row_of_strips(S_END - 4 * (NB + 1), PAIRS + 1, lambda: event_d(PAIRS - 2, NB - 3))
            row_of_strips(S_END - 4 * PAIRS, PAIRS - 1, lambda: event_d(PAIRS, NB - 2))
            event_d(PAIRS - 1, NB - 1)

        @block.tensor
        def _(pe):
            mm = nc.tensor.matmul
            pe.wait_ge(const_ready, 2)

            def turn(src, o, done):
                for m in range(OCT):
                    last = nc.tensor.transpose(turned(o)[:, m // 4, m % 4 * P:(m % 4 + 1) * P], src[:, m, :],
                                               ident[:, :])
                last.then_inc(done, 1)

            def times(w, o, dst, done):
                for m in range(OCT):
                    last = mm(dst[:, m * D:(m + 1) * D], hT[:, o % 2, m * P:(m + 1) * P], w, start=True, stop=True)
                last.then_inc(done, 1)

            def t_product(u, slot, m, leaves=None):
                if isinstance(u, int) and u in DVE_PIECES:
                    pe.wait_ge(n_lo_dve, DVE_PIECES.index(u) + 1)
                elif isinstance(u, int):
                    pe.wait_ge(n_lo_ready, u + 1 - sum(v < u for v in DVE_PIECES))
                else:
                    pe.wait_ge(n_lo_ready, u + (1 - len(DVE_PIECES)))
                for i in range(2):
                    rt = slot % CA * 8 + m * 2 + i
                    for a, low in ((n_hi, False), (n_lo, True)):
                        last = mm(fin[:, 0:CW], e_hl[:, rt, :], a[:, m, i * CW:(i + 1) * CW],
                                  start=rt == 0 and not low, stop=rt == NT - 1 and low)
                        if leaves is not None and i == 0 and not low:
                            last.then_inc(leaves, 1)
                        if rt == NT - 1 and not low:
                            last.then_inc(n_used, 1)
                if rt == NT - 1:
                    last.then_inc(t_ready, 1)
                else:
                    last.then_inc(n_used, 1)

            for step in range(NO + 3):
                o = step
                if o < NO:
                    pe.wait_ge(h0_ready, o + 1)
                    if o >= 2:
                        pe.wait_ge(h0_tc, o - 1)
                    turn(h0[:, o * OCT:(o + 1) * OCT, :], o, h0_t)
                if step == 0:
                    pe.wait_ge(par_in, 16 * 4)
                    nc.tensor.transpose(pd_row, dg_row[:, :], ident[0:NT, 0:NT]).then_inc(pd_t, 1)
                    pe.wait_ge(w_in, 64)
                o = step - 1
                if 0 <= o < NO:
                    pe.wait_ge(h0_tc, o + 1)
                    if o >= 2:
                        pe.wait_ge(e_ready, o - 1)
                    times(w_ui[:, 0 if o * OCT * P < NU else 1, :], o, psT[:, 2 + o % 2, :], h0_w)
                c = step - 3
                if 0 <= c:
                    pe.wait_ge(e_split, c + 1)
                    for m in range(NR):
                        t_product(c * NR + m, c, m)

            def t_finish(j):
                pe.wait_ge(t_copied, j)
                for i in range(2):
                    last = mm(t_rows[:, i, :], tS[:, i * P:(i + 1) * P], r_sum[:, :], start=True, stop=True)
                last.then_inc(t_row, 1)

            def transpose_a(slot, k):
                for m in range(4):
                    at = ((k // 2) * 4 + m) * CW + (k % 2) * P
                    last = nc.tensor.transpose(psT[:, k, m * P:(m + 1) * P], nat[:, slot, at:at + P], ident[:, :])
                last.then_inc(transposed, 1)

            def block_a(j, b, last_block=False, ahead_two=True):
                slot0, next0 = b * CA, (1 - b) * CA
                for q in range(SA):
                    c, k = q // 4, q % 4
                    if q == 0:
                        pe.wait_ge(t_split, j + 1)
                    pe.wait_ge(lo_ready, j * SA + q + 1)
                    ahead = not (last_block and q >= SA - 4)
                    next_slot = slot0 + c + 1 if c < CA - 1 else next0
                    if ahead:
                        transpose_a(next_slot, k)
                    bank, tile = k // 2, k % 2
                    if tile == 0:
                        pe.wait_ge(acc_free, j * 10 + q // 2 + 1)
                    first = mm(acc[:, bank, :], tT[:, b, tile, :], hi[:, k, :], start=tile == 0, stop=False)
                    if ahead and k == 3:
                        first.then_inc(slot_used[next_slot], 1)
                    mm(acc[:, bank, :], tT[:, b, tile, :], lo[:, k, :], start=False, stop=tile == 1).then_inc(strip_used, 1)
                    if not last_block:
                        if q == Q_NEXT:
                            t_finish(j + 2)
                        for n, u in pieces_beside(q):
                            if n == 1 or ahead_two:
                                t_product((j + n) * UA + u, (next0 if n == 1 else slot0) + u // NR, u % NR)

            pe.wait_ge(consts, 11)
            for k in range(4):
                transpose_a(0, k)
            t_finish(1)
            for u in range(SA - Q_NEXT):
                t_product(UA + u, CA, u, slot_used[0] if u == 0 else None)
            with pe.Fori(0, NJ // 2 - 1) as it:
                block_a(it * 2, 0)
                block_a(it * 2 + 1, 1)
            block_a(NJ - 2, 0, ahead_two=False)
            block_a(NJ - 1, 1, last_block=True)

            def transpose_b(slot, k, level=None):
                if level is not None:
                    pe.wait_ge(loaded[slot], level)
                for m in range(TB):
                    at = m * RB + k * P
                    last = nc.tensor.transpose(psT[:, k, m * P:(m + 1) * P], nat[:, slot, at:at + P], ident[:, :])
                last.then_inc(transposed, 1)

            def products(phase, j, k, bank, start, stop, leaves=None):
                n = TB * j + k
                if phase == "BX":
                    terms = [(T0_hl, hi), (T0_hl, lo)]
                elif phase == "B":
                    terms = [(vw_hi, hi), (vw_lo, hi), (vw_hi, lo)]
                elif phase == "C":
                    terms = [(uw_hi, hi), (uw_lo, hi), (uw_hi, lo)]
                else:
                    terms = [(vw_hi, hi), (vw_hi, lo)]
                for i, (v, a) in enumerate(terms):
                    last = mm(acc[:, bank, :], v[:, n], a[:, k, :], start=start and i == 0,
                              stop=stop and i == len(terms) - 1)
                    if i == 0 and leaves is not None:
                        last.then_inc(leaves, 1)
                last.then_inc(strip_used, 1)

            def finish(row, rhs, more=None):
                pe.wait_ge(acc_copied, row + 1)
                for m in range(TB):
                    tile = slice(m * P, (m + 1) * P)
                    last = mm(fin4[:, m, 0:rhs.shape[1]], accS[:, tile], rhs[:, :], start=True, stop=more is None)
                    if more is not None:
                        last = mm(fin4[:, m, more[0]], more[1][:, tile], more[2][:, :], start=False, stop=True)
                last.then_inc(fin_ready, 1)

            def finish_b(r):
                if isinstance(r, int) and r == 0:
                    finish(r, r_sum_0)
                else:
                    finish(r, r_B, (slice(0, D), accX, r_sum))

            def turn_pair(r):
                pe.wait_ge(pair_ready, r + 1)
                pe.wait_ge(fin_v, r + NB)
                pe.wait_ge(fin_a, NB)
                for m in range(TB):
                    last = nc.tensor.transpose(fin[:, m * P:(m + 1) * P], pair[:, m, :], ident[:, :])
                last.then_inc(pair_t, 1)

            def chunk(phase, j, bank, strip, ahead, level, first=False, last=False, close=None, urgent=False,
                      prior=None, pair_of=None):
                def t(k):
                    if ahead is not None:
                        pe.wait_ge(lo_ready, strip + (k + 1))
                        transpose_b(ahead, k, level if k == 0 else None)

                def p(k):
                    if ahead is None:
                        pe.wait_ge(lo_ready, strip + (k + 1))
                    leaves = None
                    if k == 3 and ahead is not None:
                        leaves = slot_used[ahead]
                    if k == 0 and prior is not None:
                        leaves = slot_used[prior]
                    products(phase, j, k, bank, first and k == 0, last and k == 3, leaves)

                t(0)
                if close is not None and urgent:
                    turn_pair(pair_of)
                    t(1)
                    close()
                    p(0)
                else:
                    p(0)
                    if pair_of is not None:
                        turn_pair(pair_of)
                    t(1)
                p(1)
                if close is not None and not urgent:
                    close()
                for k in (2, 3):
                    t(k)
                    p(k)

            def level_b(r):
                return r * 16 + 16 * (NB + 1)

            pe.wait_ge(acc_free, 10 * NJ + 2)
            for k in range(4):
                transpose_b(NB - 1, k, level_b(0) if k == 0 else None)
            for o in range(NO):
                if o >= 3:
                    pe.wait_ge(hn_ready, o - 2)
                for m in range(OCT):
                    tile = (NO - 1 - o) * OCT + m
                    last = mm(h_rows(o)[:, m * D:(m + 1) * D], hacc[:, tile * P:(tile + 1) * P], r_sum[:, :],
                              start=True, stop=True)
                last.then_inc(h_row, 1)
            for n, j in enumerate(reversed(range(NB))):
                if n % 2 == 0:
                    pe.wait_ge(T0_hi, n // 2 + 1)
                    pe.wait_ge(T0_lo, n // 2 + 1)
                ahead, r = (j - 1, 0) if j else (NB - 1, 1)
                chunk("BX", j, 1, S_B + 4 * n, ahead, level_b(r), first=n == 0, last=j == 0,
                      prior=NB - 1 if n == 0 else None)

            def row_b(r, base, close):
                def x_chunk(j, last=False, **head):
                    chunk("BX", j, 0, base + 4 * (NB - 1 - j), j - 1, level_b(r), first=j == NB - 1, last=last, **head)

                def y_chunk(j, first):
                    ahead, level = (j - 1, level_b(r)) if j else (NB - 1, level_b(r + 1))
                    chunk("B", j, 1, base + 4 * (NB - 1 - j), ahead, level, first=first, last=j == 0)

                def y_first(j):
                    pe.wait_ge(rows_ready, r)
                    pe.wait_ge(fin_v, r)
                    y_chunk(j, True)

                if isinstance(r, int):
                    x_chunk(NB - 1, close=close)
                    for j in reversed(range(r, NB - 1)):
                        x_chunk(j, last=j == r)
                    y_first(r - 1)
                    for j in reversed(range(r - 1)):
                        y_chunk(j, False)
                    return
                for j in reversed(range(NB)):
                    head = dict(close=close) if j == NB - 1 else {}
                    if j > 2:
                        with pe.If(r < j):
                            x_chunk(j, **head)
                        pe.end_ifs()
                    if j > 1:
                        with pe.If(r == j):
                            x_chunk(j, last=True, **head)
                        pe.end_ifs()
                    if 0 < j < NB - 1:
                        with pe.If(r == j + 1):
                            y_first(j)
                        pe.end_ifs()
                    if j == 0:
                        y_chunk(j, False)
                    elif j < NB - 2:
                        with pe.If(r > j + 1):
                            y_chunk(j, False)
                        pe.end_ifs()

            row_b(1, S_B + 4 * NB, lambda: finish_b(0))
            with pe.Fori(2, NB) as r:
                pe.wait_ge(x_copied, r - 1)
                row_b(r, pe.snap(r * (4 * NB) + S_B), lambda: finish_b(r - 1))

            def close_c(r):
                pe.wait_ge(pair_copied, r)
                finish(r + (NB - 1), r_C, (slice(D, 2 * D), pairT, w_01))

            pe.wait_ge(x_copied, NB - 1)
            for n, (row, j) in enumerate(head_c):
                slot = NB - 2 - n
                ahead, level = (slot, 16 * (2 * NB + 1)) if slot >= 0 else (NB - 1, 16 * (2 * NB + 2))
                head = {}
                if n == 0:
                    head = dict(close=lambda: finish_b(NB - 1))
                elif n % 2 == 0 and n <= len(LEAD):
                    head = dict(close=lambda: close_c(n // 2), urgent=n == 2, pair_of=n // 2 - 1)
                if row == j:
                    pe.wait_ge(uw_ready, 2 * j + 2)
                else:
                    pe.wait_ge(rows_ready, 2 * NB - j)
                of_row = [q for q, c in enumerate(head_c) if c[0] == row]
                chunk("C", j, 1 if row in (NB - 1, NB - 3) else 0, S_C + 4 * n, ahead, level, first=n == of_row[0],
                      last=n == of_row[-1], **head)

            def level_c(j, r):
                return r * 16 + 16 * (2 * NB + 2 - HEAD + min(0, j - (NB - 1 - HEAD)))

            with pe.Fori(HEAD // 2, PAIRS) as q:
                for b in (0, 1):
                    r = q * 2 + b
                    base = pe.snap(r * (r + 1) * 2 + S_C)

                    def more(j, **head):
                        if j < NB - 1:
                            pe.wait_ge(rows_ready, 2 * NB - j)
                        chunk("C", j, 1 - b, base + 4 * (NB - 1 - j), j - 1, level_c(j - 1, r), first=j == NB - 1,
                              **head)

                    def diagonal(j):
                        chunk("C", j, 1 - b, base + 4 * (NB - 1 - j), NB - 1, level_c(NB - 1, r + 1), last=True)

                    more(NB - 1, close=lambda: close_c(r), pair_of=r - 1)
                    for j in reversed(range(NB - HEAD - b, NB - 1)):
                        more(j)
                    for n in range(HEAD // 2, PAIRS):
                        j = NB - 1 - 2 * n - b
                        with pe.If(q == n):
                            diagonal(j)
                        pe.end_ifs()
                        if n < PAIRS - 1:
                            with pe.If(q > n):
                                more(j)
                                more(j - 1)
                            pe.end_ifs()

            def level_d(slot, m):
                return m * 16 + 16 * (used_before_d(slot) + 1)

            def close_d(n):
                if isinstance(n, int) and n == 0:
                    pe.wait_ge(fin_v, 2 * NB)
                else:
                    pe.wait_ge(out_ready, n)
                finish(n + 2 * NB, r_D)

            def long_row(m, top, close, **head):
                def diagonal(j):
                    chunk("D", j, 1, top + 4 * (NB - 1 - j), j - 1, level_d(j - 1, m), first=True, close=close,
                          **head)

                def more(j):
                    strip = top + 4 * (NB - 1 - j)
                    if j:
                        chunk("D", j, 1, strip, j - 1, level_d(j - 1, m))
                    else:
                        chunk("D", j, 1, strip, NB - 1, level_d(NB - 1, m) + 16, last=True)

                if isinstance(m, int):
                    if m == 0:
                        pe.wait_ge(t2_copied, 2)
                    diagonal(NB - 1 - m)
                    for j in reversed(range(NB - 1 - m)):
                        if m == 0:
                            pe.wait_ge(t2_copied, 2 * (NB - j))
                        more(j)
                    return
                for j in reversed(range(PAIRS + 1, NB - 1)):
                    if j < NB - 2:
                        with pe.If(m < NB - 1 - j):
                            more(j)
                        pe.end_ifs()
                    with pe.If(m == NB - 1 - j):
                        diagonal(j)
                    pe.end_ifs()
                for j in reversed(range(PAIRS + 1)):
                    more(j)

            def short_row(m, base, close):
                def more(j, **head):
                    chunk("D", j, 0, base + 4 * j, NB - 2 - j, level_d(NB - 2 - j, m) + 16, first=j == 0, **head)

                def diagonal(j, **head):
                    end = isinstance(m, int) and m == PAIRS - 1
                    ahead = NB - 2 - j
                    chunk("D", j, 0, base + 4 * j, None if end else ahead, None if end else level_d(ahead, m + 1),
                          last=True, **head)

                if isinstance(m, int):
                    if m == 0:
                        diagonal(0, first=True, close=close)
                        return
                    more(0, close=close)
                    for j in range(1, m):
                        more(j)
                    diagonal(m)
                    return
                more(0, close=close)
                for j in range(1, PAIRS - 1):
                    with pe.If(m == j):
                        diagonal(j)
                    pe.end_ifs()
                    if j < PAIRS - 2:
                        with pe.If(m > j):
                            more(j)
                        pe.end_ifs()

            long_row(0, S_D, lambda: close_c(NB), pair_of=NB - 1)
            short_row(0, S_D + 4 * NB, lambda: close_d(0))
            with pe.Fori(1, PAIRS - 1) as m:
                long_row(m, pe.snap(m * (4 * NB) + S_D), lambda: close_d(m * 2 - 1))
                short_row(m, pe.snap(m * (4 * NB) + (S_D + 4 * NB)), lambda: close_d(m * 2))
            long_row(PAIRS - 1, S_D + 4 * NB * (PAIRS - 1), lambda: close_d(NB - 3))
            short_row(PAIRS - 1, S_END - 4 * PAIRS, lambda: close_d(NB - 2))
            pe.wait_ge(out_ready, NB - 1)
            finish(3 * NB - 1, r_D)


_NAMES = ["x", "adj", "L0_gnn_W_u", "L0_gnn_diag_u", "L0_gnn_par_u", "L0_gnn_W_i", "L0_gnn_diag_i", "L0_gnn_par_i",
          "L0_gnn_ln_gamma", "L0_gnn_ln_beta", "L1_gnn_weight", "L1_gnn_bias"]


def kernel(**inputs):
    import numpy as np
    import concourse.bacc as bacc
    from concourse import mybir as mb
    from concourse.bass_utils import run_bass_kernel_spmd as run

    nc = bacc.Bacc("TRN2", target_bir_lowering=False, num_devices=1)
    arrays, args = {}, []
    for name in _NAMES:
        a = np.ascontiguousarray(inputs[name])
        arrays[f"in_{name}"] = a
        args.append(nc.dram_tensor(f"in_{name}", a.shape, mb.dt.from_np(a.dtype), kind="ExternalInput").ap())
    args.append(nc.dram_tensor("result", (N, D), F32, kind="ExternalOutput").ap())
    build(nc, *args)
    r = run(nc, [arrays], core_ids=[0])
    return r.results[0]["result"]
```
